# Optimizing a Trainium2 kernel written in Bass

```python
import numpy as np
import jax
import jax.numpy as jnp

def _softmax(x, axis=-1):
    return jax.nn.softmax(x, axis=axis)

def _gelu(x):
    return jax.nn.gelu(x, approximate=True)

def _silu(x):
    return jax.nn.silu(x)

def _sigmoid(x):
    return jax.nn.sigmoid(x)

def _layernorm(x, axis=-1, eps=1e-05):
    m = jnp.mean(x, axis=axis, keepdims=True)
    v = jnp.var(x, axis=axis, keepdims=True)
    return (x - m) / jnp.sqrt(v + eps)

def _scatter_add(tgt, idx, src, axis=0):
    return tgt.at[idx].add(src)

def _segment_sum(src, seg, n):
    return jax.ops.segment_sum(src, seg, n)
kernel_name = 'mk_audio_tower_d2_tok_aud1d768_r4_3a85e2'

def setup_inputs(seed: int=0):
    np.random.seed(seed)
    _w = jnp.asarray

    def _rec_inputs():
        import jax
        import jax.numpy as jnp
        _rk = jax.random.key(seed)
        x = -6.41493e-05 + 1.00002 * jax.random.normal(jax.random.fold_in(_rk, 1), (32, 20000), jnp.float32)
        return x
    x = _rec_inputs()

    def _L0_tok_setup():
        import jax, jax.numpy as jnp
        import numpy as np
        import math
        SR = 4000
        FRAME_LEN = 100
        FRAME_STEP = 160
        N_FILTERS = 40
        N_MFCC = 13
        EMBED = 192
        BATCH = 64
        AUDIO_LEN = 40000
        N_FFT_BINS = FRAME_LEN // 2 + 1

        def _mel_filterbank():
            low_mel = 2595.0 * math.log10(1.0 + 0.0 / 700.0)
            high_mel = 2595.0 * math.log10(1.0 + SR // 2 / 700.0)
            mel_points = np.linspace(low_mel, high_mel, N_FILTERS + 2)
            hz_points = 700.0 * (10.0 ** (mel_points / 2595.0) - 1.0)
            bin_points = np.floor((FRAME_LEN + 1) * hz_points / SR)
            filt = np.zeros((N_FILTERS, N_FFT_BINS), dtype=np.float32)
            for i in range(1, N_FILTERS + 1):
                l, c, r = (bin_points[i - 1], bin_points[i], bin_points[i + 1])
                for j in range(int(l), int(c)):
                    filt[i - 1, j] = (j - l) / (c - l)
                for j in range(int(c), int(r)):
                    filt[i - 1, j] = (r - j) / (r - c)
            return jnp.asarray(filt)

        def _dct_matrix():
            k = np.arange(N_MFCC)[:, None]
            j = np.arange(N_FILTERS)[None, :]
            m = np.cos(np.pi * k * (2 * j + 1) / (2 * N_FILTERS)) * math.sqrt(2.0 / N_FILTERS)
            return jnp.asarray(m.astype(np.float32))
        key = jax.random.key(seed)
        kx, kw = jax.random.split(key)
        x = jax.random.normal(kx, (BATCH, AUDIO_LEN), dtype=jnp.float32)
        bound = 1.0 / math.sqrt(N_MFCC)
        w_proj = jax.random.uniform(kw, (N_MFCC, EMBED), minval=-bound, maxval=bound, dtype=jnp.float32)
        b_proj = jnp.zeros((EMBED,), dtype=jnp.float32)
        return {'x': x, 'mel_filters': _mel_filterbank(), 'dct': _dct_matrix(), 'w_proj': w_proj, 'b_proj': b_proj}
    _L0_tok_all = _L0_tok_setup()
    _L0_tok_in = {k: v for k, v in _L0_tok_all.items() if k in ('mel_filters', 'dct', 'w_proj', 'b_proj')}
    del _L0_tok_all

    def _L0_attn_setup():
        import jax, jax.numpy as jnp
        import numpy as np
        B, N, DIM = (8, 256, 192)
        H, HD = (12, 64)
        INNER = H * HD
        SCALE = HD ** (-0.5)
        key = jax.random.key(seed)
        ks = jax.random.split(key, 6)
        return {'x': jax.random.normal(ks[0], (B, N, DIM), dtype=jnp.float32), 'w_qkv': jax.random.normal(ks[1], (DIM, 3 * INNER), dtype=jnp.float32) * 0.02, 'b_qkv': jax.random.normal(ks[2], (3 * INNER,), dtype=jnp.float32) * 0.02, 'reattn_weights': jax.random.normal(ks[3], (H, HD, HD), dtype=jnp.float32), 'w_out': jax.random.normal(ks[4], (INNER, DIM), dtype=jnp.float32) * 0.02, 'b_out': jax.random.normal(ks[5], (DIM,), dtype=jnp.float32) * 0.02}
    _L0_attn_all = _L0_attn_setup()
    _L0_attn_in = {k: v for k, v in _L0_attn_all.items() if k in ('w_qkv', 'b_qkv', 'reattn_weights', 'w_out', 'b_out')}
    del _L0_attn_all

    def _L0_ffn_setup():
        import jax, jax.numpy as jnp
        import numpy as np
        DIM = 192
        FF = 768
        E = 8
        K = 2
        H = 12
        HD = DIM // H
        LN_EPS = 1e-05

        def _layernorm(x, g, b):
            m = jnp.mean(x, axis=-1, keepdims=True)
            v = jnp.var(x, axis=-1, keepdims=True)
            return (x - m) * jax.lax.rsqrt(v + LN_EPS) * g + b

        def _attention(x, Wqkv, Wproj):
            B, T, D = x.shape
            qkv = (x @ Wqkv).reshape(B, T, 3, H, HD)
            q, k, v = (qkv[:, :, 0], qkv[:, :, 1], qkv[:, :, 2])
            scores = jnp.einsum('bqhd,bkhd->bhqk', q, k) * jnp.float32(HD) ** (-0.5)
            attn = jax.nn.softmax(scores, axis=-1)
            out = jnp.einsum('bhqk,bkhd->bqhd', attn, v).reshape(B, T, D)
            return out @ Wproj

        def _moe(x, Wrouter, W1, W2):
            B, T, D = x.shape
            xf = x.reshape(-1, D)
            N = xf.shape[0]
            logits = xf @ Wrouter
            topk_w, topk_idx = jax.lax.top_k(logits, K)
            topk_w = jax.nn.softmax(topk_w.astype(jnp.float32), axis=-1).astype(x.dtype)
            we = jnp.zeros((N, E), x.dtype).at[jnp.arange(N)[:, None], topk_idx].add(topk_w)

            def body(acc, expert):
                W1e, W2e, we_e = expert
                h = jax.nn.gelu(xf @ W1e, approximate=False)
                return (acc + we_e[:, None] * (h @ W2e), None)
            out, _ = jax.lax.scan(body, jnp.zeros_like(xf), (W1, W2, we.T))
            return out.reshape(B, T, D)
        key = jax.random.key(seed)
        ks = jax.random.split(key, 7)
        B, T = (4, 256)
        init = lambda k, shape, fan: jax.random.normal(k, shape, jnp.float32) * fan ** (-0.5)
        return {'x': jax.random.normal(ks[0], (B, T, DIM), jnp.float32), 'Wqkv': init(ks[1], (DIM, 3 * DIM), DIM), 'Wproj': init(ks[2], (DIM, DIM), DIM), 'Wrouter': init(ks[3], (DIM, E), DIM), 'W1': init(ks[4], (E, DIM, FF), DIM), 'W2': init(ks[5], (E, FF, DIM), FF), 'ln1_g': jnp.ones((DIM,), jnp.float32), 'ln1_b': jnp.zeros((DIM,), jnp.float32), 'ln2_g': jnp.ones((DIM,), jnp.float32), 'ln2_b': jnp.zeros((DIM,), jnp.float32)}
    _L0_ffn_all = _L0_ffn_setup()
    _L0_ffn_in = {k: v for k, v in _L0_ffn_all.items() if k in ('Wqkv', 'Wproj', 'Wrouter', 'W1', 'W2', 'ln1_g', 'ln1_b', 'ln2_g', 'ln2_b')}
    del _L0_ffn_all

    def _L1_attn_setup():
        import jax, jax.numpy as jnp
        import numpy as np
        B, T, D = (2, 1024, 192)
        H, HD = (6, D // 6)
        key = jax.random.key(seed)
        ks = jax.random.split(key, 8)
        s = 0.02
        return {'x': jax.random.normal(ks[0], (B, T, D), dtype=jnp.float32), 'Wq': jax.random.normal(ks[1], (D, D), dtype=jnp.float32) * s, 'Wk': jax.random.normal(ks[2], (D, D), dtype=jnp.float32) * s, 'Wv': jax.random.normal(ks[3], (D, D), dtype=jnp.float32) * s, 'Wo': jax.random.normal(ks[4], (D, D), dtype=jnp.float32) * s, 'anchor_w': jax.random.normal(ks[5], (H, HD, 6), dtype=jnp.float32) * s, 'anchors': jnp.sign(jax.random.normal(ks[6], (H, 6), dtype=jnp.float32)), 'lam': jnp.full((H,), 0.1, dtype=jnp.float32)}
    _L1_attn_all = _L1_attn_setup()
    _L1_attn_in = {k: v for k, v in _L1_attn_all.items() if k in ('Wq', 'Wk', 'Wv', 'Wo', 'anchor_w', 'anchors', 'lam')}
    del _L1_attn_all

    def _L1_ffn_setup():
        import jax, jax.numpy as jnp
        import numpy as np
        GT0 = [[0, 1, 0, 0, 1, 0], [0, 1, 0, 0, 0, 1], [0, 0, 1, 0, 1, 0], [0, 0, 1, 0, 0, 1], [0, 0, 0, 1, 1, 0], [0, 0, 0, 1, 0, 1]]
        NCLS = 6
        K = 1

        def _expert_pairs():
            pairs = []
            for i in range(NCLS):
                p = [(j - 1, k - 1) for j in range(1, 6) for k in range(1, 6) if j != k and GT0[i][j] == 1 and (GT0[i][k] == 1)]
                pairs.append(p)
            return pairs
        PAIRS = _expert_pairs()
        B, P, D, H = (64, 64, 192, 768)

        def _gelu(t):
            return jax.nn.gelu(t, approximate=False)
        key = jax.random.key(seed)
        ks = jax.random.split(key, 8)
        s = 0.02
        x = jax.random.normal(ks[0], (B, NCLS + P, D), dtype=jnp.float32)
        mids = jax.random.randint(ks[1], (B,), 0, 6)
        moe0_W1 = jax.random.normal(ks[2], (D, H), dtype=jnp.float32) * s
        moe0_b1 = jnp.zeros((H,), jnp.float32)
        moe0_W2 = jax.random.normal(ks[3], (H, D), dtype=jnp.float32) * s
        moe0_b2 = jnp.zeros((D,), jnp.float32)
        A1_W = jax.random.normal(ks[4], (5, D, H), dtype=jnp.float32) * s
        A1_b = jnp.zeros((5, H), jnp.float32)
        A2_W = jax.random.normal(ks[5], (5, H, D), dtype=jnp.float32) * s
        A2_b = jnp.zeros((5, D), jnp.float32)
        G_W = jax.random.normal(ks[6], (NCLS, D, 2), dtype=jnp.float32) * s
        return {'x': x, 'moe0_W1': moe0_W1, 'moe0_b1': moe0_b1, 'moe0_W2': moe0_W2, 'moe0_b2': moe0_b2, 'A1_W': A1_W, 'A1_b': A1_b, 'A2_W': A2_W, 'A2_b': A2_b, 'G_W': G_W, 'mids': mids}
    _L1_ffn_all = _L1_ffn_setup()
    _L1_ffn_in = {k: v for k, v in _L1_ffn_all.items() if k in ('moe0_W1', 'moe0_b1', 'moe0_W2', 'moe0_b2', 'A1_W', 'A1_b', 'A2_W', 'A2_b', 'G_W', 'mids')}
    del _L1_ffn_all
    return {'x': x, 'L0_tok_mel_filters': _L0_tok_in['mel_filters'], 'L0_tok_dct': _L0_tok_in['dct'], 'L0_tok_w_proj': _L0_tok_in['w_proj'], 'L0_tok_b_proj': _L0_tok_in['b_proj'], 'L0_attn_w_qkv': _L0_attn_in['w_qkv'], 'L0_attn_b_qkv': _L0_attn_in['b_qkv'], 'L0_attn_reattn_weights': _L0_attn_in['reattn_weights'], 'L0_attn_w_out': _L0_attn_in['w_out'], 'L0_attn_b_out': _L0_attn_in['b_out'], 'L0_ffn_Wqkv': _L0_ffn_in['Wqkv'], 'L0_ffn_Wproj': _L0_ffn_in['Wproj'], 'L0_ffn_Wrouter': _L0_ffn_in['Wrouter'], 'L0_ffn_W1': _L0_ffn_in['W1'], 'L0_ffn_W2': _L0_ffn_in['W2'], 'L0_ffn_ln1_g': _L0_ffn_in['ln1_g'], 'L0_ffn_ln1_b': _L0_ffn_in['ln1_b'], 'L0_ffn_ln2_g': _L0_ffn_in['ln2_g'], 'L0_ffn_ln2_b': _L0_ffn_in['ln2_b'], 'L1_attn_Wq': _L1_attn_in['Wq'], 'L1_attn_Wk': _L1_attn_in['Wk'], 'L1_attn_Wv': _L1_attn_in['Wv'], 'L1_attn_Wo': _L1_attn_in['Wo'], 'L1_attn_anchor_w': _L1_attn_in['anchor_w'], 'L1_attn_anchors': _L1_attn_in['anchors'], 'L1_attn_lam': _L1_attn_in['lam'], 'L1_ffn_moe0_W1': _L1_ffn_in['moe0_W1'], 'L1_ffn_moe0_b1': _L1_ffn_in['moe0_b1'], 'L1_ffn_moe0_W2': _L1_ffn_in['moe0_W2'], 'L1_ffn_moe0_b2': _L1_ffn_in['moe0_b2'], 'L1_ffn_A1_W': _L1_ffn_in['A1_W'], 'L1_ffn_A1_b': _L1_ffn_in['A1_b'], 'L1_ffn_A2_W': _L1_ffn_in['A2_W'], 'L1_ffn_A2_b': _L1_ffn_in['A2_b'], 'L1_ffn_G_W': _L1_ffn_in['G_W'], 'L1_ffn_mids': _L1_ffn_in['mids']}

def reference(x, L0_tok_mel_filters, L0_tok_dct, L0_tok_w_proj, L0_tok_b_proj, L0_attn_w_qkv, L0_attn_b_qkv, L0_attn_reattn_weights, L0_attn_w_out, L0_attn_b_out, L0_ffn_Wqkv, L0_ffn_Wproj, L0_ffn_Wrouter, L0_ffn_W1, L0_ffn_W2, L0_ffn_ln1_g, L0_ffn_ln1_b, L0_ffn_ln2_g, L0_ffn_ln2_b, L1_attn_Wq, L1_attn_Wk, L1_attn_Wv, L1_attn_Wo, L1_attn_anchor_w, L1_attn_anchors, L1_attn_lam, L1_ffn_moe0_W1, L1_ffn_moe0_b1, L1_ffn_moe0_W2, L1_ffn_moe0_b2, L1_ffn_A1_W, L1_ffn_A1_b, L1_ffn_A2_W, L1_ffn_A2_b, L1_ffn_G_W, L1_ffn_mids):
    import jax
    import jax.numpy as jnp

    def _L0_tok_ref(x, mel_filters, dct, w_proj, b_proj):
        import jax, jax.numpy as jnp
        import numpy as np
        import math
        SR = 4000
        FRAME_LEN = 100
        FRAME_STEP = 160
        N_FILTERS = 40
        N_MFCC = 13
        EMBED = 192
        BATCH = 64
        AUDIO_LEN = 40000
        N_FFT_BINS = FRAME_LEN // 2 + 1

        def _mel_filterbank():
            low_mel = 2595.0 * math.log10(1.0 + 0.0 / 700.0)
            high_mel = 2595.0 * math.log10(1.0 + SR // 2 / 700.0)
            mel_points = np.linspace(low_mel, high_mel, N_FILTERS + 2)
            hz_points = 700.0 * (10.0 ** (mel_points / 2595.0) - 1.0)
            bin_points = np.floor((FRAME_LEN + 1) * hz_points / SR)
            filt = np.zeros((N_FILTERS, N_FFT_BINS), dtype=np.float32)
            for i in range(1, N_FILTERS + 1):
                l, c, r = (bin_points[i - 1], bin_points[i], bin_points[i + 1])
                for j in range(int(l), int(c)):
                    filt[i - 1, j] = (j - l) / (c - l)
                for j in range(int(c), int(r)):
                    filt[i - 1, j] = (r - j) / (r - c)
            return jnp.asarray(filt)

        def _dct_matrix():
            k = np.arange(N_MFCC)[:, None]
            j = np.arange(N_FILTERS)[None, :]
            m = np.cos(np.pi * k * (2 * j + 1) / (2 * N_FILTERS)) * math.sqrt(2.0 / N_FILTERS)
            return jnp.asarray(m.astype(np.float32))
        B, T = x.shape
        n_frames = 1 + (T - FRAME_LEN) // FRAME_STEP
        idx = jnp.arange(n_frames)[:, None] * FRAME_STEP + jnp.arange(FRAME_LEN)[None, :]
        frames = x[:, idx]
        window = 0.54 - 0.46 * jnp.cos(2.0 * jnp.pi * jnp.arange(FRAME_LEN, dtype=jnp.float32) / (FRAME_LEN - 1))
        windowed = frames * window
        fft = jnp.fft.rfft(windowed, axis=-1)
        power = fft.real ** 2 + fft.imag ** 2
        mel_energies = jnp.einsum('bnf,mf->bnm', power, mel_filters)
        log_energies = jnp.log(mel_energies + 1e-06)
        mfcc = jnp.einsum('bnm,km->bnk', log_energies, dct)
        out = mfcc @ w_proj + b_proj
        return out

    def _L0_attn_ref(x, w_qkv, b_qkv, reattn_weights, w_out, b_out):
        import jax, jax.numpy as jnp
        import numpy as np
        B, N, DIM = (8, 256, 192)
        H, HD = (12, 64)
        INNER = H * HD
        SCALE = HD ** (-0.5)
        b, n, _ = x.shape
        qkv = x @ w_qkv + b_qkv
        q, k, v = jnp.split(qkv, 3, axis=-1)

        def to_heads(t):
            return t.reshape(b, n, H, HD).transpose(0, 2, 1, 3)
        q, k, v = (to_heads(q), to_heads(k), to_heads(v))
        dots = jnp.einsum('bhid,bhjd->bhij', q, k) * SCALE
        attn = jax.nn.softmax(dots, axis=-1)
        head_scale = reattn_weights.sum(axis=(-1, -2))
        attn = attn * head_scale[None, :, None, None]
        out = jnp.einsum('bhij,bhjd->bhid', attn, v)
        out = out.transpose(0, 2, 1, 3).reshape(b, n, INNER)
        return out @ w_out + b_out

    def _L0_ffn_ref(x, Wqkv, Wproj, Wrouter, W1, W2, ln1_g, ln1_b, ln2_g, ln2_b):
        import jax, jax.numpy as jnp
        import numpy as np
        DIM = 192
        FF = 768
        E = 8
        K = 2
        H = 12
        HD = DIM // H
        LN_EPS = 1e-05

        def _layernorm(x, g, b):
            m = jnp.mean(x, axis=-1, keepdims=True)
            v = jnp.var(x, axis=-1, keepdims=True)
            return (x - m) * jax.lax.rsqrt(v + LN_EPS) * g + b

        def _attention(x, Wqkv, Wproj):
            B, T, D = x.shape
            qkv = (x @ Wqkv).reshape(B, T, 3, H, HD)
            q, k, v = (qkv[:, :, 0], qkv[:, :, 1], qkv[:, :, 2])
            scores = jnp.einsum('bqhd,bkhd->bhqk', q, k) * jnp.float32(HD) ** (-0.5)
            attn = jax.nn.softmax(scores, axis=-1)
            out = jnp.einsum('bhqk,bkhd->bqhd', attn, v).reshape(B, T, D)
            return out @ Wproj

        def _moe(x, Wrouter, W1, W2):
            B, T, D = x.shape
            xf = x.reshape(-1, D)
            N = xf.shape[0]
            logits = xf @ Wrouter
            topk_w, topk_idx = jax.lax.top_k(logits, K)
            topk_w = jax.nn.softmax(topk_w.astype(jnp.float32), axis=-1).astype(x.dtype)
            we = jnp.zeros((N, E), x.dtype).at[jnp.arange(N)[:, None], topk_idx].add(topk_w)

            def body(acc, expert):
                W1e, W2e, we_e = expert
                h = jax.nn.gelu(xf @ W1e, approximate=False)
                return (acc + we_e[:, None] * (h @ W2e), None)
            out, _ = jax.lax.scan(body, jnp.zeros_like(xf), (W1, W2, we.T))
            return out.reshape(B, T, D)
        x = x + _attention(_layernorm(x, ln1_g, ln1_b), Wqkv, Wproj)
        x = x + _moe(_layernorm(x, ln2_g, ln2_b), Wrouter, W1, W2)
        return x

    def _L1_attn_ref(x, Wq, Wk, Wv, Wo, anchor_w, anchors, lam):
        import jax, jax.numpy as jnp
        import numpy as np
        B, T, D = (2, 1024, 192)
        H, HD = (6, D // 6)
        b, t, d = x.shape
        scale = HD ** (-0.5)
        q = (x @ Wq.T).reshape(b, t, H, HD).transpose(0, 2, 1, 3)
        k = (x @ Wk.T).reshape(b, t, H, HD).transpose(0, 2, 1, 3)
        v = (x @ Wv.T).reshape(b, t, H, HD).transpose(0, 2, 1, 3)
        scores = jnp.einsum('bhqd,bhkd->bhqk', q, k) * scale
        anchor_h = jnp.einsum('hde,he->hd', anchor_w, anchors)
        anchor_sim = jnp.einsum('bhtd,hd->bht', q, anchor_h)
        scores = scores + (lam[None, :, None] * anchor_sim)[..., None]
        attn = jax.nn.softmax(scores, axis=-1)
        out = jnp.einsum('bhqk,bhkd->bhqd', attn, v)
        out = out.transpose(0, 2, 1, 3).reshape(b, t, d)
        return out @ Wo.T

    def _L1_ffn_ref(x, moe0_W1, moe0_b1, moe0_W2, moe0_b2, A1_W, A1_b, A2_W, A2_b, G_W, mids):
        import jax, jax.numpy as jnp
        import numpy as np
        GT0 = [[0, 1, 0, 0, 1, 0], [0, 1, 0, 0, 0, 1], [0, 0, 1, 0, 1, 0], [0, 0, 1, 0, 0, 1], [0, 0, 0, 1, 1, 0], [0, 0, 0, 1, 0, 1]]
        NCLS = 6
        K = 1

        def _expert_pairs():
            pairs = []
            for i in range(NCLS):
                p = [(j - 1, k - 1) for j in range(1, 6) for k in range(1, 6) if j != k and GT0[i][j] == 1 and (GT0[i][k] == 1)]
                pairs.append(p)
            return pairs
        PAIRS = _expert_pairs()
        B, P, D, H = (64, 64, 192, 768)

        def _gelu(t):
            return jax.nn.gelu(t, approximate=False)
        cls_tokens = x[:, :NCLS]
        patch_tokens = x[:, NCLS:]
        patch_out = _gelu(patch_tokens @ moe0_W1 + moe0_b1) @ moe0_W2 + moe0_b2
        cls_outs = []
        for i in range(NCLS):
            tok = cls_tokens[:, i]
            eouts = [_gelu(tok @ A1_W[a] + A1_b[a]) @ A2_W[c] + A2_b[c] for a, c in PAIRS[i]]
            out = jnp.stack(eouts, axis=-1)
            gate = jax.nn.softmax(tok @ G_W[i], axis=-1)
            thr = jnp.sort(gate, axis=-1)[..., -(K + 1)]
            mask = (gate > thr[..., None]).astype(gate.dtype)
            g = gate * mask
            g = g / jnp.clip(jnp.sum(g, axis=-1, keepdims=True), 1e-06)
            cls_outs.append(jnp.sum(out * g[:, None, :], axis=-1))
        cls_out = jnp.stack(cls_outs, axis=1)
        return jnp.concatenate([cls_out, patch_out], axis=1)
    h = _L0_tok_ref(x, L0_tok_mel_filters, L0_tok_dct, L0_tok_w_proj, L0_tok_b_proj)
    h = h + _L0_attn_ref(_layernorm(h, axis=-1), L0_attn_w_qkv, L0_attn_b_qkv, L0_attn_reattn_weights, L0_attn_w_out, L0_attn_b_out)
    h = h + _L0_ffn_ref(_layernorm(h, axis=-1), L0_ffn_Wqkv, L0_ffn_Wproj, L0_ffn_Wrouter, L0_ffn_W1, L0_ffn_W2, L0_ffn_ln1_g, L0_ffn_ln1_b, L0_ffn_ln2_g, L0_ffn_ln2_b)
    h = h + _L1_attn_ref(_layernorm(h, axis=-1), L1_attn_Wq, L1_attn_Wk, L1_attn_Wv, L1_attn_Wo, L1_attn_anchor_w, L1_attn_anchors, L1_attn_lam)
    h = h + _L1_ffn_ref(_layernorm(h, axis=-1), L1_ffn_moe0_W1, L1_ffn_moe0_b1, L1_ffn_moe0_W2, L1_ffn_moe0_b2, L1_ffn_A1_W, L1_ffn_A1_b, L1_ffn_A2_W, L1_ffn_A2_b, L1_ffn_G_W, L1_ffn_mids)
    return h

_drawn_inputs = setup_inputs


def setup_inputs(seed=0):
    import zlib

    import numpy as np

    out = dict(_drawn_inputs(seed))
    spreads = {'L0_tok_b_proj': (0.0, 0.319),
     'L0_ffn_ln1_g': (1.0, 0.55),
     'L0_ffn_ln1_b': (0.0, 0.595),
     'L0_ffn_ln2_g': (1.0, 0.6),
     'L0_ffn_ln2_b': (0.0, 0.687),
     'L1_attn_lam': (0.10000000149011612, 0.6),
     'L1_ffn_moe0_b1': (0.0, 0.8),
     'L1_ffn_moe0_b2': (0.0, 0.8),
     'L1_ffn_A1_b': (0.0, 0.8),
     'L1_ffn_A2_b': (0.0, 2.0)}
    factors = {'L0_attn_b_out': 21.861,
     'L1_attn_Wq': 64.0,
     'L1_attn_Wk': 64.0,
     'L1_attn_Wv': 7.746,
     'L1_attn_Wo': 6.587,
     'L1_attn_anchor_w': 64.0,
     'L1_attn_anchors': 64.0,
     'L1_ffn_moe0_W1': 7.449,
     'L1_ffn_moe0_W2': 7.339,
     'L1_ffn_A1_W': 8.0,
     'L1_ffn_A2_W': 8.0,
     'L1_ffn_G_W': 8.0}
    for name, (base, spread) in spreads.items():
        noise = np.random.default_rng([zlib.crc32(name.encode()), seed]).standard_normal(out[name].shape)
        drawn = base * np.exp(spread * noise) if base else spread * noise
        out[name] = jnp.asarray(drawn.astype(out[name].dtype))
    for name, factor in factors.items():
        out[name] = (out[name] * factor).astype(out[name].dtype)
    return out
```

```python
from contextlib import ExitStack

import numpy as np

import concourse.bass as bass
from concourse import mybir

F32 = mybir.dt.float32
I32 = mybir.dt.int32
U32 = mybir.dt.uint32
ALU = mybir.AluOpType
ACT = mybir.ActivationFunctionType
AX = mybir.AxisListType

CLIPS, SAMPLES = 32, 20000
FRAME, STEP = 100, 160
T = 1 + (SAMPLES - FRAME) // STEP
BINS = FRAME // 2 + 1
MELS, MFCC = 40, 13
D = 192
DA, DB = 128, D - 128
NB = 4
GROUPS = CLIPS // NB
GT = NB * T
FF = 768
FJ = FF // 128
E = 8
TOKENS = CLIPS * T
REGION = TOKENS + 128
TILES = (2 * TOKENS - E) // 128 + E
AHEAD = 2
LOADED = 2 * AHEAD
EPS_LN = 1e-5
NCLS = 6
NEXP = 5
PAIR = [(0, 3), (0, 4), (1, 3), (1, 4), (2, 3), (2, 4)]
SERVES = [[i for i in range(NCLS) if e in PAIR[i]] for e in range(NEXP)]


class Attn:

    def __init__(self, index, heads, hd, slot, n, owners):
        self.index, self.heads, self.hd, self.slot, self.n = index, heads, hd, slot, n
        per = 128 // slot
        self.tiles = [min(per, heads - t * per) * slot for t in range(-(-heads // per))]
        self.qk = sum(self.tiles)
        self.inner = heads * hd
        self.halves = 2 if self.inner > 512 else 1
        self.owners = owners
        names = list(owners)
        clip = [n for n in names if n[0] in "xqkv"]
        self.slots = ([["q0"], ["k0"], ["q1", "k1"], ["v0"], ["v1"]] if self.halves == 2 else
                      [["q"], ["k"], [], ["v"], []])
        body = [(b, n) for b in range(NB) for n in clip]
        first = list(body)
        last = [x for x in body if x[0] < NB - 1]
        tail = []
        if index == 1:
            def routed(body):
                body = list(body)
                body[body.index((2, "v")):body.index((2, "v"))] = [(2, "ra"), (2, "rb")]
                body.insert(body.index((2, "v")) + 1, (2, "lg"))
                body.insert(body.index((3, "v")) if (3, "v") in body else len(body), (3, "ct"))
                return body
            body, last = routed(body), routed(last)
            tail = [(2, "ra"), (2, "rb"), (2, "lg"), (3, "ct")]
        self.order = {"start": [(0, n) for n in clip], "first": first, "mid": body, "last": last, "tail": tail}
        assert len(body) % 2 == 0
        self.before = (0, 0, 0)

    def count(self, fills):
        own = [self.owners[n] for _, n in fills]
        return np.array([len(own), own.count("dve"), own.count("act")])

    def base(self, place, g):
        o = self.order
        upto = np.array(self.before)
        if place == "start":
            return upto, 0 * upto
        upto = upto + self.count(o["start"])
        if place == "first":
            return upto, 0 * upto
        upto = upto + self.count(o["first"])
        mid = self.count(o["mid"])
        if place == "mid":
            return upto - mid, mid
        upto = upto + mid * (GROUPS - 2)
        if place == "last":
            return upto, 0 * upto
        return upto + self.count(o["last"]), 0 * upto

    def total(self):
        return self.base("tail", 0)[0] + self.count(self.order["tail"])

    def head(self, unit, bank, i):
        if self.index == 0:
            tile, rg = 3 * unit + i, bank
        else:
            tile, rg = i, 2 * unit + bank
        return tile * (128 // self.slot) + rg, tile, rg * self.slot

    def osb_view(self, osb, unit):
        n = self.n[unit]
        if self.index == 0:
            v = osb[0:T, 0:768].rearrange("p (i k d) -> p k i d", k=2, d=self.hd)
            return v[:, :, 3 * unit:3 * unit + 3, :]
        v = osb[0:T, 0:4 * self.hd * 3].rearrange("p (i u k d) -> p u k i d", u=2, k=2, d=self.hd)
        return v[:, unit, :, 0:n, :]


class Chain:

    def __init__(self, eng, sem):
        self.eng, self.sem, self.base, self.n, self.i, self.per = eng, sem, 0, 0, None, 0

    def enter(self, i, per, start=0):
        self.i, self.n, self.per, self.start = i, 0, per, start

    def leave(self, trips):
        assert self.n == self.per, (self.n, self.per)
        self.base, self.i = self.base + trips * self.per, None

    def after(self, ins):
        ins.then_inc(self.sem, 1)
        self.n += 1
        if self.i is None:
            self.base += 1
            self.eng.wait_ge(self.sem, self.base)
        else:
            self.eng.wait_ge(self.sem, self.base - self.start * self.per + self.i * self.per + self.n)


def wait(eng, sem, count):
    if not isinstance(count, (int, np.integer)) or count > 0:
        eng.wait_ge(sem, int(count) if isinstance(count, np.integer) else count)


def layers():
    owners = [
        dict(x="dve", q0="act", k0="dve", q1="act", k1="dve", v0="dve", v1="dve"),
        dict(x="dve", q="act", k="act", v="act", ra="dve", rb="act", lg="dve", ct="dve"),
        dict(x="dve", q="act", k="dve", v="act"),
    ]
    out, before = [], np.zeros(3, int)
    for i, (heads, hd, slot, n) in enumerate([(12, 64, 64, [3, 3]), (12, 16, 32, [3, 3]), (6, 32, 32, [2, 1])]):
        a = Attn(i, heads, hd, slot, n, owners[i])
        a.before = before
        before = a.total()
        out.append(a)
    return out


LAYERS = layers()
CHAIN = [17, 40, 19, 2]
CHAIN_POOL = [1, 3, 1, 1]
UNITS = 2 * NB


def constants():
    c = {}
    c["ident"] = np.eye(128)
    c["before"] = np.triu(np.ones((128, 128)), 1)
    c["ones"] = np.ones((128, 128))
    e = np.arange(E)
    c["rev"] = np.tile(E - e, (128, NB))
    c["region"] = np.tile(e * REGION, (128, 1))
    c["bounds"] = np.tile(np.tile(128 * np.arange(32), E), (128, 1))
    t = np.arange(TILES + LOADED)
    c["tile"] = np.tile(np.repeat(t, E), (128, 1))
    c["tile_e"] = np.tile(np.tile(e, TILES + LOADED), (128, 1))
    c["pair"] = np.kron(np.eye(2), np.ones((64, 64)))
    c["tiny"] = np.full((128, 1), 1e-6)
    c["eps"] = np.full((128, NB), EPS_LN)
    c["half"] = np.full((128, 4), -0.5)
    return {k: np.asarray(v, np.float32) for k, v in c.items()}


def const_columns():
    at, out = 0, {}
    for k, v in constants().items():
        out[k] = (at, v.shape[1])
        at += v.shape[1]
    return out, at


def build(nc, A, out):
    cols, ncols = const_columns()
    with ExitStack() as ctx:
        def sb(name, shape, dt=F32):
            return ctx.enter_context(nc.sbuf_tensor(name, shape, dt))

        def sem(name):
            return ctx.enter_context(nc.semaphore(name))

        routed = nc.dram_tensor("routed_rows", (E * REGION, D), F32).ap()
        expert_out = nc.dram_tensor("expert_rows", (TILES * 128, D), F32).ap()

        cst = sb("cst", [128, ncols])
        hid = sb("hid", [128, CLIPS, D])
        rows = sb("rows", [128, 2 * D + 768])
        region1 = sb("region1", [128, 2 * E * FF])
        region2 = sb("region2", [128, E * FJ * D])
        region3 = sb("region3", [128, 13712])
        xn = sb("xn", [128, NB, D])
        xTa = sb("xTa", [DA, GT])
        xTb = sb("xTb", [DB, GT])
        w_l1 = sb("w_l1", [128, 2 * 960 + 2 * D])
        colsm = sb("colsm", [128, 64])
        stats = sb("stats", [128, NB, 6])
        mv = sb("mv", [128, NB, 2])
        rstd = sb("rstd", [128, NB])
        mx = sb("mx", [128, 2, 6])
        rsum = sb("rsum", [128, 2, 6])
        smallw = sb("smallw", [128, 640])
        route = sb("route", [128, 12 * NB * E])
        hot = sb("hot", [128, 2, CLIPS, E])
        gap = sb("gap", [128, CLIPS])
        pos = sb("pos", [128, 2, CLIPS])
        wgt = sb("wgt", [128, 2, CLIPS])
        run = sb("run", [128, E])
        spread = sb("spread", [128, E * 32])
        tl = sb("tl", [128, 4, E])
        tab = sb("tab", [1, 2, TILES + LOADED], I32)
        padrow = sb("padrow", [1, E], I32)
        idx = sb("idx", [128, 2, NB], U32)
        idy = sb("idy", [128, 2, NB], U32)
        zeros = sb("zeros", [128, D])
        rstd2 = sb("rstd2", [128, NB])
        kept = sb("kept", [128, 2 * NB])
        nudge = sb("nudge", [1, 8])
        shift = sb("shift", [128, CLIPS])

        ps = ctx.enter_context(nc.psum_tensor("ps", [128, 8, 512], F32))

        def const(name, p=128):
            a, n = cols[name]
            return cst[0:p, a:a + n]

        ident = const("ident")

        w0a = region2[:, 0:2304]
        w0b = region2[0:DB, 2304:4608]
        wo0 = region2[:, 4608:5760].rearrange("p (j n) -> p j n", j=6)
        QT = region3[:, 0:750].rearrange("p (m t) -> p m t", t=T)
        KT = region3[:, 750:1500].rearrange("p (m t) -> p m t", t=T)
        Vr = region3[:, 1500:2280]
        Pr = region3[:, 2280:3780].rearrange("p (b x) -> p b x", b=2)
        PTr = region3[:, 3780:5280].rearrange("p (b x) -> p b x", b=2)
        osb = region3[:, 5280:6048]
        OT = region3[:, 6048:6798].rearrange("p (j t) -> p j t", t=T)
        rTa = region3[:, 1710:1710 + GT]
        rTb = region3[0:DB, 5480:5480 + GT]
        xres = region3[:, 6800:6800 + CLIPS * D].rearrange("p (b d) -> p b d", b=CLIPS)
        xrow = region3[:, 12944:12944 + NB * D].rearrange("p (b d) -> p b d", b=NB)
        w_l2 = region3[:, 6800:6800 + 1536]
        got = region3[:, 8400:8400 + 8 * D].rearrange("p (s b d) -> p s b d", s=2, b=NB)
        tabf = region3[0:1, 10000:10000 + 3 * (TILES + LOADED) * E].rearrange("p (k x) -> p k x", k=3)
        LW = [
            (w0a, w0b, [wo0[:, j, :] for j in range(6)]),
            (w_l1[:, 0:960], w_l1[0:DB, 960:1920], [w_l1[:, 1920:2112], w_l1[0:DB, 2112:2304]]),
            (w_l2[:, 0:576], w_l2[0:DB, 576:1152], [w_l2[:, 1152:1344], w_l2[0:DB, 1344:1536]]),
        ]
        frames = region3[0:FRAME, 0:TOKENS]
        power = region3[0:2 * BINS, 4000:4000 + GT]
        logmel = region3[0:MELS, 4500:4500 + GT]
        melw = smallw[0:2 * BINS, 0:MELS]
        dct = smallw[0:MFCC, 40:80]
        wproj = smallw[0:MFCC, 80:272]
        combined = smallw[0:MELS, 272:464]
        dft = smallw[0:FRAME, 464:464 + 2 * BINS]
        M0 = 0
        xs = region3[:, M0:M0 + 384].rearrange("p (b d) -> p b d", b=2)
        xsT = region3[:, M0 + 384:M0 + 896].rearrange("p (b x) -> p b x", b=2)
        act1 = region3[:, M0 + 896:M0 + 2432].rearrange("p (b x) -> p b x", b=2)
        act1T = region3[:, M0 + 2432:M0 + 3968].rearrange("p (b x) -> p b x", b=2)
        ys = region3[:, M0 + 3968:M0 + 4352].rearrange("p (b d) -> p b d", b=2)
        m1a = region1[:, 0:E * FF]
        m1b = region1[0:DB, E * FF:2 * E * FF]
        m2 = region2[:, :]
        a1a = region1[:, 0:NEXP * FF]
        a1b = region1[0:DB, NEXP * FF:2 * NEXP * FF]
        f1a = region1[:, 7680:7680 + FF]
        f1b = region1[0:DB, 7680 + FF:7680 + 2 * FF]
        f2 = region1[:, 9216:9216 + FJ * D]
        a2 = region2[:, 0:NEXP * FJ * D]
        rows2 = region2[:, 5760:5760 + (1 + NEXP) * D]
        actF = region3[:, 0:6 * GT].rearrange("p (j t) -> p j t", j=FJ)
        fin = region3[:, 3000:3000 + NB * D].rearrange("p (b d) -> p b d", b=NB)
        clsa = region3[:, 3800:3800 + NCLS * CLIPS].rearrange("p (i b) -> p i b", i=NCLS)
        clsb = region3[0:DB, 4000:4000 + NCLS * CLIPS].rearrange("p (i b) -> p i b", i=NCLS)
        clsh = region3[0:CLIPS, 4200:4200 + NCLS * D].rearrange("p (i d) -> p i d", i=NCLS)
        clsact = region3[:, 5400:5400 + NEXP * FJ * 96].rearrange("p (e j x) -> p e j x", e=NEXP, j=FJ)
        clso = region3[0:CLIPS, 8300:8300 + 2 * NCLS * D].rearrange("p (i s d) -> p i s d", i=NCLS, s=2)
        gate = region3[0:CLIPS, 10700:10800]
        b1c = region3[:, 10800:10806]
        a1bc = region3[:, 10806:10836]
        gwa = region3[:, 10840:10852]
        gwb = region3[0:DB, 10860:10872]

        def column(a, n=1, p=128):
            return colsm[0:p, a:a + n]

        BQ, BK, LN_A, LN_B, HSC, ROUT_A, ROUT_B, ANC = 0, 6, 12, 16, 20, 26, 34, 42

        s_const = sem("consts_loaded")
        s_tokw = sem("token_weights_loaded")
        s_frames = sem("frames_loaded")
        s_w0 = sem("layer0_weights_loaded")
        s_cols = sem("columns_loaded")
        s_w1 = sem("layer1_weights_loaded")
        s_w2 = sem("layer2_weights_loaded")
        s_m1 = sem("mixture_w1_loaded")
        s_m2 = sem("mixture_w2_loaded")
        s_f1 = sem("last_w1_loaded")
        s_f2 = sem("last_w2_loaded")
        s_reat = sem("head_weights_loaded")
        s_anc = sem("anchors_loaded")
        s_set = sem("setup_done_by_vector")
        s_setp = sem("setup_done_by_pool")
        s_comb = sem("mfcc_projection_in_psum")
        s_hsum = sem("head_sums_in_psum")
        s_dft = sem("spectrum_in_psum")
        s_pow = sem("power_in_sbuf")
        s_mel = sem("mel_in_psum")
        s_log = sem("logmel_in_sbuf")
        s_tok = sem("tokens_in_psum")
        s_hid = sem("tokens_in_hid")
        s_dve = sem("vector_chain")
        s_poolc = sem("pool_chain")
        s_var = sem("variances_ready")
        s_xn = sem("normalized_rows_ready")
        s_rstd = sem("reciprocal_deviations_ready")
        s_res = sem("bias_added_to_residual")
        s_x = sem("projection_bank_full")
        s_xd = sem("projection_taken_by_vector")
        s_xc = sem("projection_taken_by_scalar")
        s_s = sem("scores_in_psum")
        s_sub = sem("scores_less_max")
        s_exp = sem("probs_ready")
        s_pt = sem("probs_transposed_in_psum")
        s_ptc = sem("probs_transposed_in_sbuf")
        s_o = sem("heads_out_in_psum")
        s_on = sem("heads_out_normalized")
        s_ot = sem("heads_out_transposed_in_psum")
        s_otc = sem("heads_out_transposed_in_sbuf")
        s_y = sem("attention_out_in_psum")
        s_hup = sem("attention_out_taken")
        s_r = sem("routing_matmuls_done")
        s_rt = sem("routing_bank_taken")
        s_hot = sem("one_hots_ready")
        s_idx = sem("scatter_rows_ready")
        s_scat = [sem(f"rows_scattered_{k}") for k in range(2 * NB)]
        s_tab = sem("tile_tables_ready")
        s_pad = sem("pad_rows_written")
        s_gexp = sem("gap_exponential_ready")
        s_wgt = sem("mixture_weights_ready")
        s_ld = [sem(f"tile_loaded_{k}") for k in range(2)]
        s_mt = sem("tile_transposed_in_psum")
        s_mtc = sem("tile_transposed_in_sbuf")
        s_m1p = sem("expert_hidden_in_psum")
        s_gel = sem("expert_gelu_ready")
        s_gt = sem("expert_gelu_transposed_in_psum")
        s_gtc = sem("expert_gelu_transposed_in_sbuf")
        s_m2p = sem("expert_out_in_psum")
        s_ys = sem("expert_out_in_sbuf")
        s_st = [sem(f"tile_stored_{k}") for k in range(2)]
        s_idy = sem("gather_rows_ready")
        s_got = [sem(f"expert_rows_gathered_{k}") for k in range(2 * NB)]
        s_mix = sem("mixture_added")
        s_fh = sem("last_hidden_in_psum")
        s_fg = sem("last_gelu_ready")
        s_fy = sem("last_out_in_psum")
        s_ft = sem("last_out_taken")
        s_lx = sem("last_rows_transposed_in_psum")
        s_lxd = sem("last_rows_taken_by_vector")
        s_lxc = sem("last_rows_taken_by_scalar")
        s_out = sem("output_stored")
        s_clsh = sem("class_rows_moved")
        s_cls = sem("class_columns_kept")
        s_ch = sem("class_hidden_in_psum")
        s_cg = sem("class_gelu_ready")
        s_cgate = sem("class_gates_in_psum")
        s_cge = sem("class_gate_exponentials")
        s_csub = sem("class_gate_less_max")
        s_cy = sem("class_out_in_psum")
        s_ct = sem("class_out_taken")
        s_cfin = sem("class_rows_ready")
        s_cout = sem("class_rows_stored")
        s_lnd = sem("second_norm_rows_ready")

        block = ctx.enter_context(nc.Block())

        def settled(eng, place=0):
            if eng is nc.vector:
                return nc.vector.memset(nudge[0:1, 0:1], 0.0)
            return nc.gpsimd.tensor_tensor(nudge[0:1, 1 + place:2 + place], const("half", 1)[:, 0:1], const("half", 1)[:, 0:1], ALU.add)

        def fill(a, place, b, name):
            k = a.order[place].index((b, name))
            return k, 2 + int(a.base(place, 0)[0][0] + k) % 2

        def filled(eng, a, place, g, b, name):
            base, per = a.base(place, g)
            eng.wait_ge(s_x, int(base[0]) + fill(a, place, b, name)[0] + 1 + (int(per[0]) * g if per[0] else 0))

        def taken_upto(eng, a, place, g, k, who):
            base, per = a.base(place, g)
            n = int(base[who])
            if k >= 0:
                n += int(a.count(a.order[place][:k + 1])[who])
            elif k == -2:
                n -= int(a.count([(0, clip_fills(a)[-1])])[who])
            wait(eng, (None, s_xd, s_xc)[who], n + (int(per[who]) * g if per[who] else 0))

        def clip_fills(a):
            return [n for _, n in a.order["start"]]

        def bank_free(eng, a, place, g, b, name):
            k = fill(a, place, b, name)[0] - 2
            if k >= 0:
                took(eng, a, place, g, *a.order[place][k])
            else:
                for who in (1, 2):
                    taken_upto(eng, a, place, g, k, who)

        def took(eng, a, place, g, b, name):
            taken_upto(eng, a, place, g, fill(a, place, b, name)[0], 1 if a.owners[name] == "dve" else 2)

        def took_last(eng, a, place, g, b, name):
            if b > 0:
                took(eng, a, place, g, b - 1, name)
            elif place == "first":
                took(eng, a, "start", 0, 0, name)
            else:
                names = clip_fills(a)
                later = a.count([(0, n) for n in names[names.index(name) + 1:]])
                if name in "xqk":
                    later = later + a.count([(3, "ct")]) * (a.index == 1)
                base, per = a.base(place, g)
                who = 1 if a.owners[name] == "dve" else 2
                n = int(base[who]) - int(later[who])
                eng.wait_ge((None, s_xd, s_xc)[who], n + (int(per[who]) * g if per[who] else 0))

        NORMS = [0, GROUPS, 4 * GROUPS, 5 * GROUPS]

        def norm(a, place, g, which):
            n = NORMS[a.index]
            if a.index != 1:
                return n + (1 if place == "start" else g + 2)
            if place == "start":
                return n + dict(own=1, next=2)[which]
            if place == "first":
                return n + dict(own=3, next=4)[which]
            if place == "mid":
                return n + 3 * g + dict(own=2, route=3, next=4)[which]
            return n + 3 * (GROUPS - 1) + (2 if place == "last" else 3)

        def norm_of(a, place, g):
            if place == "start" or place == "first":
                return norm(a, "start", 0, "next")
            if a.index != 1:
                return NORMS[a.index] + g + 1
            return NORMS[1] + 3 * g + 1

        def routed_group(place, g):
            return GROUPS - 1 if place == "tail" else g - 1

        def vview(a):
            return Vr[0:T, 0:a.heads * (a.hd + 1)].rearrange("p (h x) -> p h x", h=a.heads)

        def scores_view(a, s):
            n = a.n[s % 2]
            return ps[0:T, 0:2, 0:n * T].rearrange("p k (i t) -> p k i t", i=n)

        def probs(a, s):
            n = a.n[s % 2]
            return Pr[0:T, s % 2, 0:2 * n * T].rearrange("p (k i t) -> p k i t", k=2, i=n)

        def probsT(a, s):
            n = a.n[s % 2]
            return PTr[0:T, s % 2, 0:2 * n * T].rearrange("p (k x) -> p k x", k=2)

        def heads_out(a, s):
            n = a.n[s % 2]
            return ps[0:T, 6, 0:2 * n * (a.hd + 1)].rearrange("p (k i x) -> p k i x", k=2, i=n)

        def out_runs(a):
            return [(c, min(128, a.inner - c)) for c in range(0, a.inner, 128)]

        def tiles_of(a, name):
            if a.halves == 2:
                return range(3 * int(name[1]), 3 * int(name[1]) + 3)
            return range(len(a.tiles))

        def following(b):
            return (b + 1) // NB, (b + 1) % NB


        @block.sync
        def _(sp):
            sp.dma_start(cst[:, :], A["consts"]).then_inc(s_const, 16)
            sp.dma_start(melw, A["melw"]).then_inc(s_tokw, 16)
            sp.dma_start(dct, A["dct"]).then_inc(s_tokw, 16)
            sp.dma_start(wproj, A["wproj"]).then_inc(s_tokw, 16)
            sp.dma_start(dft, A["dft"]).then_inc(s_tokw, 16)
            sp.dma_start(frames, A["frames"]).then_inc(s_frames, 16)
            sp.dma_start(rows[:, :], A["rows"].partition_broadcast(128)).then_inc(s_cols, 16)
            sp.dma_start(colsm[:, 0:42], A["cols"]).then_inc(s_cols, 16)
            sp.dma_start(region1[:, 0:384], A["reat"]).then_inc(s_reat, 16)
            sp.dma_start(region1[:, 384:384 + 28], A["anchor"]).then_inc(s_anc, 16)
            sp.dma_start(w0a, A["w0a"]).then_inc(s_w0, 16)
            sp.dma_start(w0b, A["w0b"]).then_inc(s_w0, 16)
            sp.dma_start(region2[:, 4608:5760], A["wo0"]).then_inc(s_w0, 16)
            sp.dma_start(w_l1[:, :], A["w1"]).then_inc(s_w1, 16)
            sp.wait_ge(s_set, 1)
            sp.dma_start(m1a, A["m1a"]).then_inc(s_m1, 16)
            sp.dma_start(m1b, A["m1b"]).then_inc(s_m1, 16)
            sp.wait_ge(s_hup, CLIPS)
            sp.dma_start(m2, A["m2"]).then_inc(s_m2, 16)
            sp.wait_ge(s_res, 2 * GROUPS)
            for k in range(2 * NB):
                sp.wait_ge(s_scat[k], 16 * GROUPS)
            sp.dma_start(w_l2, A["w2"]).then_inc(s_w2, 16)

            sp.wait_ge(s_tab, 1)
            sp.wait_ge(s_setp, 1)
            for e in range(E):
                r = sp.value_load(padrow[0:1, e:e + 1], min_val=0, max_val=E * REGION - 128)
                sp.dma_start(routed[bass.ds(r, 128), :], zeros[:, :]).then_inc(s_pad, 16)
            sp.wait_ge(s_pad, 16 * E)

            def load_tile(t, par):
                r = sp.value_load(tab[0:1, 0, bass.ds(t, 1)], min_val=0, max_val=E * REGION - 128)
                sp.dma_start(xs[:, par, :], routed[bass.ds(r, 128), :]).then_inc(s_ld[par], 16)

            load_tile(0, 0)
            load_tile(1, 1)
            for par in range(2):
                sp.wait_ge(s_mt, par + 1)
                load_tile(AHEAD + par, par)
            with sp.Fori(0, TILES // 2) as i:
                for par in range(2):
                    sp.wait_ge(s_mt, 2 * i + par + AHEAD + 1)
                    load_tile(2 * i + par + LOADED, par)
                    sp.wait_ge(s_ys, 2 * i + par + 1)
                    sp.dma_start(expert_out[bass.ds((2 * i + par) * 128, 128), :],
                                 ys[:, par, :]).then_inc(s_st[par], 16)
            for par in range(2):
                sp.wait_ge(s_ld[par], 16 * (TILES + LOADED) // 2)

            sp.wait_ge(s_m2p, TILES)
            sp.dma_start(region1[:, 0:7680], A["a1"]).then_inc(s_f1, 16)
            sp.dma_start(region1[:, 7680:7680 + 2 * FF + FJ * D], A["f"]).then_inc(s_f1, 16)
            sp.dma_start(a2, A["a2"]).then_inc(s_f2, 16)
            sp.dma_start(rows2, A["rows2"].partition_broadcast(128)).then_inc(s_f2, 16)
            sp.wait_ge(s_hup, 3 * CLIPS)
            sp.dma_start(region3[:, 10800:10880], A["lastcols"]).then_inc(s_f2, 16)
            for i in range(NCLS):
                sp.dma_start(clsh[:, i, :], hid[i:i + 1, :, :]).then_inc(s_clsh, 16)
            with sp.Fori(0, GROUPS) as g:
                sp.wait_ge(s_ft, NB * (g + 1))
                sp.dma_start(out[bass.ds(g * NB, NB), NCLS:T, :].rearrange("b n d -> n b d"),
                             fin[NCLS:T, :, :]).then_inc(s_out, 16)
            sp.wait_ge(s_cfin, NCLS)
            sp.dma_start(out[:, 0:NCLS, :], clsh).then_inc(s_cout, 16)
            sp.wait_ge(s_out, 16 * GROUPS)
            sp.wait_ge(s_cout, 16)
            for k in range(2):
                sp.wait_ge(s_st[k], 16 * (TILES // 2))

        def mixture_tensor(pe, mm):
            pe.wait_ge(s_m1, 32)
            pe.wait_ge(s_m2, 16)
            pe.wait_ge(s_tab, 1)

            def turn_rows(par, i):
                pe.wait_ge(s_ld[par], 16 * (i + 1))
                nc.tensor.transpose(ps[:, 0, 0:128], xs[:, par, 0:DA], ident)
                nc.tensor.transpose(ps[0:DB, 0, 128:256], xs[:, par, DA:D], ident).then_inc(s_mt, 1)

            def expert_of(t):
                return pe.value_load(tab[0:1, 1, bass.ds(t, 1)], min_val=0, max_val=E - 1)

            def hidden(par, half, e):
                o = ps[:, 1 + 2 * par + half, 0:384]
                mm(o, xsT[:, par, 0:128], m1a[:, bass.ds(e * FF + half * 384, 384)], True, False)
                last = mm(o, xsT[0:DB, par, 128:256], m1b[:, bass.ds(e * FF + half * 384, 384)], False, True)
                if half:
                    last.then_inc(s_m1p, 1)

            def tile(i, par):
                t = 2 * i + par
                e = expert_of(t + 1)
                pe.wait_ge(s_mtc, t + 2)
                wait(pe, s_gel, t)
                hidden(1 - par, 0, e)
                turn_rows(par, i + 1)
                pe.wait_ge(s_gel, t + 1)
                wait(pe, s_gtc, t)
                for j in range(FJ):
                    last = nc.tensor.transpose(ps[:, 5 + j // 3, (j % 3) * 128:(j % 3 + 1) * 128],
                                               act1[:, par, j * 128:(j + 1) * 128], ident)
                last.then_inc(s_gt, 1)
                hidden(1 - par, 1, e)
                e = expert_of(t)
                pe.wait_ge(s_gtc, t + 1)
                wait(pe, s_ys, t)
                for j in range(FJ):
                    last = mm(ps[:, 7, 0:D], act1T[:, par, j * 128:(j + 1) * 128],
                              m2[:, bass.ds(e * (FJ * D) + j * D, D)], j == 0, j == FJ - 1)
                last.then_inc(s_m2p, 1)

            turn_rows(0, 0)
            pe.wait_ge(s_mtc, 1)
            turn_rows(1, 0)
            e = expert_of(0)
            hidden(0, 0, e)
            hidden(0, 1, e)
            tile(0, 0)
            tile(0, 1)
            with pe.Fori(1, TILES // 2) as i:
                tile(i, 0)
                tile(i, 1)

        @block.tensor
        def _(pe):
            def mm(o, lhsT, rhs, first=True, last=True):
                return nc.tensor.matmul(o, lhsT, rhs, start=first, stop=last)

            pe.wait_ge(s_const, 16)
            pe.wait_ge(s_tokw, 64)
            mm(ps[0:MELS, 7, 0:D], dct, wproj).then_inc(s_comb, 1)
            pe.wait_ge(s_set, 1)
            mm(ps[:, 6, 0:6], const("pair"), column(HSC, 6)).then_inc(s_hsum, 1)

            pe.wait_ge(s_set, 2)
            pe.wait_ge(s_frames, 16)
            with pe.Fori(0, GROUPS) as g:
                mm(ps[0:2 * BINS, 0, 0:GT], dft, frames[:, bass.ds(g * GT, GT)]).then_inc(s_dft, 1)
                pe.wait_ge(s_pow, g + 1)
                mm(ps[0:MELS, 1, 0:GT], melw, power).then_inc(s_mel, 1)
                pe.wait_ge(s_log, g + 1)
                pe.wait_ge(s_hid, g)
                for b in range(NB):
                    last = mm(ps[0:T, 2 + b // 2, (b % 2) * D:(b % 2 + 1) * D],
                              logmel[:, b * T:(b + 1) * T], combined)
                last.then_inc(s_tok, 1)

            def project(a, place, g, b, name):
                bank = fill(a, place, b, name)[1]
                wa, wb, _ = LW[a.index]
                if name == "ra":
                    bank_free(pe, a, place, g, b, "rb")
                if name != "rb":
                    bank_free(pe, a, place, g, b, name)
                xa, xb = xTa[:, 0:T], xTb[:, 0:T]
                if name == "x":
                    later, at = (0, 0) if place == "start" else following(b)
                    pe.wait_ge(s_xn, norm(a, place, g, "next") if later else norm_of(a, place, g))
                    nc.tensor.transpose(ps[0:DA, bank, 0:T], xn[0:T, at, 0:DA], ident[0:T, 0:T])
                    last = nc.tensor.transpose(ps[0:DB, bank, 128:128 + T], xn[0:T, at, DA:D], ident[0:T, 0:T])
                elif name[0] in "qk":
                    took(pe, a, place, g, b, "x")
                    for j, tile in enumerate(tiles_of(a, name)):
                        c = 128 * tile + (a.qk if name[0] == "k" else 0)
                        w = a.tiles[tile]
                        o = ps[0:w, bank, j * T:(j + 1) * T]
                        mm(o, wa[:, c:c + w], xa, True, False)
                        last = mm(o, wb[:, c:c + w], xb, False, True)
                elif name[0] == "v":
                    w = a.inner // a.halves
                    c = 2 * a.qk + (int(name[1]) * w if a.halves == 2 else 0)
                    o = ps[0:T, bank, 0:w]
                    mm(o, xa, wa[:, c:c + w], True, False)
                    last = mm(o, xb, wb[:, c:c + w], False, True)
                elif name in ("ra", "rb"):
                    if name == "ra":
                        pe.wait_ge(s_xn, norm(a, place, g, "route"))
                    c, w = (0, DA) if name == "ra" else (DA, DB)
                    for i in range(NB):
                        last = nc.tensor.transpose(ps[0:w, bank, i * T:(i + 1) * T],
                                                   xrow[0:T, i, c:c + w], ident[0:T, 0:T])
                elif name == "lg":
                    took(pe, a, place, g, 2, "ra")
                    took(pe, a, place, g, 2, "rb")
                    for i in range(NB):
                        o = ps[0:T, bank, i * E:(i + 1) * E]
                        mm(o, rTa[:, i * T:(i + 1) * T], column(ROUT_A, E), True, False)
                        last = mm(o, rTb[:, i * T:(i + 1) * T], column(ROUT_B, E, DB), False, True)
                else:
                    pe.wait_ge(s_hot, routed_group(place, g) + 1)
                    picked = route[0:T, 0:NB * E]
                    mm(ps[0:T, bank, 0:NB * E], const("before", T)[:, 0:T], picked)
                    last = mm(ps[0:T, bank, NB * E:2 * NB * E], const("ones", T)[:, 0:T], picked)
                last.then_inc(s_x, 1)

            def scores(a, place, g, s):
                step = (a.index * GROUPS + g) * UNITS
                b = s // 2
                for kind in "qk":
                    name = kind + str(s % 2) if a.halves == 2 else kind
                    if place == "start":
                        took(pe, a, place, g, 0, name)
                    elif a.halves == 2 or s % 2 == 0:
                        took_last(pe, a, place, g, b, name)
                wait(pe, s_sub, step + s)
                for i in range(a.n[s % 2]):
                    for k in range(2):
                        _, tile, p = a.head(s % 2, k, i)
                        last = mm(ps[0:T, k, i * T:(i + 1) * T],
                                  QT[p:p + a.hd, tile, :], KT[p:p + a.hd, tile, :])
                last.then_inc(s_s, 1)

            def clip_body(a, place, g, b, more):
                step = (a.index * GROUPS + g) * UNITS
                clip = (a.index * GROUPS + g) * NB

                def probs_transposed(s):
                    pe.wait_ge(s_exp, step + s + 1)
                    wait(pe, s_ptc, step + s)
                    if s % 2 == 0:
                        wait(pe, s_otc, clip + b)
                    for k in range(2):
                        for i in range(a.n[s % 2]):
                            last = nc.tensor.transpose(ps[0:T, 4 + k, i * T:(i + 1) * T],
                                                       probs(a, s)[:, k, i, :], ident[0:T, 0:T])
                    last.then_inc(s_pt, 1)

                def heads(s):
                    pe.wait_ge(s_ptc, step + s + 1)
                    wait(pe, s_on, step + s)
                    if s % 2 == 0:
                        for name in clip_fills(a):
                            if name[0] == "v":
                                took_last(pe, a, place, g, b, name)
                    for k in range(2):
                        for i in range(a.n[s % 2]):
                            h, _, _ = a.head(s % 2, k, i)
                            last = mm(heads_out(a, s)[:, k, i, :], probsT(a, s)[:, k, i * T:(i + 1) * T],
                                      vview(a)[:, h, :])
                    last.then_inc(s_o, 1)

                def projections(slot):
                    for name in a.slots[slot] if more else []:
                        project(a, place, g, b, name)

                s = 2 * b
                probs_transposed(s)
                if more:
                    project(a, place, g, b, "x")
                scores(a, place, g, s + 1)
                projections(0)
                heads(s)
                projections(1)
                probs_transposed(s + 1)
                projections(2)
                routing = a.index == 1 and place != "first"
                if routing and b == 2:
                    project(a, place, g, b, "ra")
                    project(a, place, g, b, "rb")
                if routing and b == 3:
                    project(a, place, g, b, "ct")
                if more:
                    scores(a, place, g, s + 2)
                heads(s + 1)
                projections(3)
                pe.wait_ge(s_on, step + s + 2)
                for j, (c, w) in enumerate(out_runs(a)):
                    last = nc.tensor.transpose(ps[0:w, 4 + j // 3, (j % 3) * T:(j % 3 + 1) * T],
                                               osb[0:T, c:c + w], ident[0:T, 0:T])
                last.then_inc(s_ot, 1)
                projections(4)
                if routing and b == 2:
                    project(a, place, g, b, "lg")
                pe.wait_ge(s_otc, clip + b + 1)
                wait(pe, s_hup, clip + b)
                for j, (c, w) in enumerate(out_runs(a)):
                    last = mm(ps[0:T, 7, 0:D], OT[0:w, j, :], LW[a.index][2][j], j == 0, c + w == a.inner)
                last.then_inc(s_y, 1)

            for a, loaded, n in ((LAYERS[0], s_w0, 48), (LAYERS[1], s_w1, 16), (LAYERS[2], s_w2, 16)):
                pe.wait_ge(loaded, n)
                if a.index == 0:
                    pe.wait_ge(s_set, 3)
                    pe.wait_ge(s_hid, GROUPS)
                if a.index == 2:
                    mixture_tensor(pe, mm)
                    pe.wait_ge(s_gel, TILES)
                    pe.wait_ge(s_gtc, TILES)
                    pe.wait_ge(s_ys, TILES)
                for name in clip_fills(a):
                    project(a, "start", 0, 0, name)
                scores(a, "start", 0, 0)
                for b in range(NB):
                    clip_body(a, "first", 0, b, True)
                with pe.Fori(1, GROUPS - 1) as g:
                    for b in range(NB):
                        clip_body(a, "mid", g, b, True)
                for b in range(NB):
                    clip_body(a, "last", GROUPS - 1, b, b < NB - 1)
                for b, name in a.order["tail"]:
                    project(a, "tail", GROUPS - 1, b, name)

            pe.wait_ge(s_f1, 32)
            pe.wait_ge(s_f2, 48)
            pe.wait_ge(s_hup, 3 * CLIPS)

            def turned(g):
                pe.wait_ge(s_xn, NORMS[3] + g + 1)
                for k, c, w in ((0, 0, DA), (1, DA, DB)):
                    for b in range(NB):
                        last = nc.tensor.transpose(ps[0:w, 4 + k, b * T:(b + 1) * T],
                                                   xn[0:T, b, c:c + w], ident[0:T, 0:T])
                last.then_inc(s_lx, 1)

            def last_group(g, more):
                pe.wait_ge(s_lxd, g + 1)
                for j in range(FJ):
                    wait(pe, s_fg, g * FJ + j - 1)
                    mm(ps[:, j % 2, 0:GT], f1a[:, j * 128:(j + 1) * 128], xTa[:, :], True, False)
                    mm(ps[:, j % 2, 0:GT], f1b[:, j * 128:(j + 1) * 128], xTb[:, :], False, True).then_inc(s_fh, 1)
                if more:
                    turned(g + 1)
                pe.wait_ge(s_fg, g * FJ + FJ)
                for b in range(NB):
                    wait(pe, s_ft, g * NB + b - 1)
                    for j in range(FJ):
                        last = mm(ps[0:T, 6 + b % 2, 0:D], actF[:, j, b * T:(b + 1) * T],
                                  f2[:, j * D:(j + 1) * D], j == 0, j == FJ - 1)
                    last.then_inc(s_fy, 1)

            turned(0)
            last_group(0, True)
            with pe.Fori(1, GROUPS - 1) as g:
                last_group(g, True)
            last_group(GROUPS - 1, False)

            pe.wait_ge(s_cls, GROUPS)
            for i in range(NCLS):
                mm(ps[0:CLIPS, 4, 2 * i:2 * i + 2], clsa[:, i, :], gwa[:, 2 * i:2 * i + 2], True, False)
                last = mm(ps[0:CLIPS, 4, 2 * i:2 * i + 2], clsb[:, i, :], gwb[:, 2 * i:2 * i + 2], False, True)
            last.then_inc(s_cgate, 1)
            for e in range(NEXP):
                if e >= 2:
                    pe.wait_ge(s_cg, e - 1)
                first, step = SERVES[e][0], SERVES[e][1] - SERVES[e][0]
                n = len(SERVES[e])
                for j in range(FJ):
                    o = ps[:, 2 * (e % 2) + j // 3, (j % 3) * 96:(j % 3) * 96 + n * CLIPS]
                    stop = first + step * (n - 1) + 1
                    c = e * FF + j * 128
                    mm(o, a1a[:, c:c + 128], clsa[:, first:stop:step, :], True, False)
                    last = mm(o, a1b[:, c:c + 128], clsb[:, first:stop:step, :], False, True)
                last.then_inc(s_ch, 1)
            pe.wait_ge(s_cg, NEXP)
            pe.wait_ge(s_ft, CLIPS)
            for i in range(NCLS):
                if i >= 2:
                    pe.wait_ge(s_ct, i - 1)
                for s in range(2):
                    e, f = PAIR[i][s], PAIR[i][1 - s]
                    at = SERVES[e].index(i) * CLIPS
                    for j in range(FJ):
                        c = (f * FJ + j) * D
                        last = mm(ps[0:CLIPS, 6 + i % 2, s * D:(s + 1) * D], clsact[:, e, j, at:at + CLIPS],
                                  a2[:, c:c + D], j == 0, j == FJ - 1)
                last.then_inc(s_cy, 1)

        @block.scalar
        def _(act):
            act.wait_ge(s_const, 16)
            with act.Fori(0, GROUPS) as g:
                act.wait_ge(s_dft, g + 1)
                nc.scalar.activation(power, ps[0:2 * BINS, 0, 0:GT], ACT.Square).then_inc(s_pow, 1)
                act.wait_ge(s_mel, g + 1)
                nc.scalar.activation(logmel, ps[0:MELS, 1, 0:GT], ACT.Ln,
                                     bias=const("tiny", MELS)).then_inc(s_log, 1)

            def evict(a, place, g, b, name):
                if a.owners[name] != "act":
                    return
                bank = fill(a, place, b, name)[1]
                filled(act, a, place, g, b, name)
                if name == "rb":
                    last = nc.scalar.activation(rTb, ps[0:DB, bank, 0:GT], ACT.Identity,
                                                scale=column(LN_B + 2, 1, DB), bias=column(LN_B + 3, 1, DB))
                elif name[0] in "qk":
                    dst = QT if name[0] == "q" else KT
                    tiles = tiles_of(a, name)
                    if a.index == 1:
                        last = nc.scalar.copy(dst[:, 0:3, :].rearrange("p m t -> p (m t)"), ps[:, bank, 0:3 * T])
                    else:
                        for j, tile in enumerate(tiles):
                            w = a.tiles[tile]
                            src = ps[0:w, bank, j * T:(j + 1) * T]
                            if a.index == 0:
                                last = nc.scalar.activation(QT[:, tile, :], src, ACT.Identity,
                                                            bias=column(BQ + tile))
                            else:
                                last = nc.scalar.copy(dst[0:w, tile, :], src)
                else:
                    src = ps[0:T, bank, 0:a.inner].rearrange("p (h x) -> p h x", h=a.heads)
                    last = nc.scalar.copy(vview(a)[:, :, 0:a.hd], src)
                last.then_inc(s_xc, 1)

            def exp(a, g, s):
                step = (a.index * GROUPS + g) * UNITS
                act.wait_ge(s_sub, step + s + 1)
                p = Pr[0:T, s % 2, 0:2 * a.n[s % 2] * T]
                nc.scalar.activation(p, p, ACT.Exp,
                                     scale=1.0 if a.index == 2 else float(a.hd) ** -0.5).then_inc(s_exp, 1)

            def clip_body(a, place, g, b, more):
                step = (a.index * GROUPS + g) * UNITS
                clip = (a.index * GROUPS + g) * NB

                def evictions(slot):
                    for name in a.slots[slot] if more else []:
                        evict(a, place, g, b, name)

                def probs_copied(s):
                    act.wait_ge(s_pt, step + s + 1)
                    wait(act, s_o, step + s - 1)
                    nc.scalar.copy(probsT(a, s), ps[0:T, 4:6, 0:a.n[s % 2] * T]).then_inc(s_ptc, 1)

                s = 2 * b
                probs_copied(s)
                evictions(0)
                exp(a, g, s + 1)
                evictions(1)
                probs_copied(s + 1)
                evictions(2)
                if a.index == 1 and place != "first" and b == 2:
                    evict(a, place, g, b, "rb")
                evictions(3)
                act.wait_ge(s_ot, clip + b + 1)
                wait(act, s_y, clip + b)
                if a.index == 0:
                    o = OT[:, :, :].rearrange("p (k j) t -> p k (j t)", k=2)
                    last = nc.scalar.copy(o, ps[:, 4:6, 0:3 * T])
                else:
                    for j, (_, w) in enumerate(out_runs(a)):
                        last = nc.scalar.copy(OT[0:w, j, :], ps[0:w, 4, j * T:(j + 1) * T])
                last.then_inc(s_otc, 1)
                evictions(4)
                if more:
                    exp(a, g, s + 2)

            def gelu_tile(i, par):
                t = 2 * i + par
                act.wait_ge(s_m1p, t + 1)
                nc.scalar.activation(act1[:, par, :].rearrange("p (k x) -> p k x", k=2),
                                     ps[:, 1 + 2 * par:3 + 2 * par, 0:384], ACT.Gelu).then_inc(s_gel, 1)

            for a in LAYERS:
                if a.index == 0:
                    act.wait_ge(s_cols, 32)
                if a.index == 2:
                    act.wait_ge(s_tab, 1)
                    nc.scalar.activation(wgt[0:T, 1, :], gap[0:T, :], ACT.Exp).then_inc(s_gexp, 1)
                    with act.Fori(0, TILES // 2) as i:
                        gelu_tile(i, 0)
                        gelu_tile(i, 1)
                for name in clip_fills(a):
                    evict(a, "start", 0, 0, name)
                exp(a, 0, 0)
                for b in range(NB):
                    clip_body(a, "first", 0, b, True)
                with act.Fori(1, GROUPS - 1) as g:
                    for b in range(NB):
                        clip_body(a, "mid", g, b, True)
                for b in range(NB):
                    clip_body(a, "last", GROUPS - 1, b, b < NB - 1)
                for b, name in a.order["tail"]:
                    evict(a, "tail", GROUPS - 1, b, name)

            act.wait_ge(s_f2, 48)
            with act.Fori(0, GROUPS) as g:
                for j in range(FJ):
                    act.wait_ge(s_fh, g * FJ + j + 1)
                    nc.scalar.activation(actF[:, j, :], ps[:, j % 2, 0:GT], ACT.Gelu,
                                         bias=b1c[:, j:j + 1]).then_inc(s_fg, 1)
            for e in range(NEXP):
                act.wait_ge(s_ch, e + 1)
                n = len(SERVES[e]) * CLIPS
                for j in range(FJ):
                    last = nc.scalar.activation(clsact[:, e, j, 0:n],
                                                ps[:, 2 * (e % 2) + j // 3, (j % 3) * 96:(j % 3) * 96 + n],
                                                ACT.Gelu, bias=a1bc[:, e * FJ + j:e * FJ + j + 1])
                last.then_inc(s_cg, 1)
            act.wait_ge(s_csub, 1)
            nc.scalar.activation(gate[:, 16:28], gate[:, 0:12], ACT.Exp).then_inc(s_cge, 1)

        @block.vector
        def _(dve):
            ch = Chain(dve, s_dve)
            V = nc.vector

            dve.wait_ge(s_cols, 32)
            dve.wait_ge(s_reat, 16)
            dve.wait_ge(s_anc, 16)
            for t in range(2):
                c = 384 + 14 * t
                prod = region1[:, 416 + 8 * t:422 + 8 * t]
                ch.after(V.tensor_tensor(prod, region1[:, c:c + 6], region1[:, c + 6:c + 12], ALU.mult))
                ch.after(V.tensor_reduce(mx[:, 0, t:t + 1], prod, AX.X, ALU.add))
                V.tensor_tensor(column(ANC + t), mx[:, 0, t:t + 1], region1[:, c + 12:c + 13], ALU.mult)
            V.tensor_reduce(column(HSC, 6), region1[:, 0:384].rearrange("p (j c) -> p j c", j=6),
                            AX.X, ALU.add).then_inc(s_set, 1)
            dve.wait_ge(s_comb, 1)
            V.tensor_copy(combined, ps[0:MELS, 7, 0:D]).then_inc(s_set, 1)
            dve.wait_ge(s_hsum, 1)
            ch.after(V.tensor_copy(rsum[:, 0, :], ps[:, 6, 0:6]))
            dve.wait_ge(s_w0, 48)
            V.tensor_tensor(wo0, wo0, rsum[:, 0, :].unsqueeze(2).to_broadcast([128, 6, D]),
                            ALU.mult).then_inc(s_set, 1)
            dve.wait_ge(s_const, 16)
            V.tensor_copy(run[:, :], const("region"))

            with dve.Fori(0, GROUPS) as g:
                dve.wait_ge(s_tok, g + 1)
                for c in range(2):
                    last = V.tensor_tensor(hid[0:T, bass.ds(g * NB + 2 * c, 2), :],
                                           ps[0:T, 2 + c, 0:2 * D].rearrange("p (b d) -> p b d", b=2),
                                           rows[0:T, 0:D].unsqueeze(1).to_broadcast([T, 2, D]), ALU.add)
                last.then_inc(s_hid, 1)

            def measure(count, src):
                wait(dve, s_xn, count - 1)
                settled(nc.vector)
                for b in range(NB):
                    last = V.bn_stats(stats[0:T, b, :], src(b))
                ch.after(last)
                settled(nc.vector)
                for b in range(NB):
                    last = V.bn_aggr(mv[0:T, b, :], stats[0:T, b, :])
                last.then_inc(s_var, 1)

            def apply(count, src, dst):
                dve.wait_ge(s_rstd, count)
                for b in range(NB):
                    last = V.tensor_scalar(dst(b), src(b), mv[0:T, b, 0:1], rstd[0:T, b:b + 1],
                                           ALU.subtract, ALU.mult)
                last.then_inc(s_xn, 1)

            def hid_of(g):
                return lambda b: hid[0:T, g * NB + b, :]

            def xres_of(g):
                return lambda b: xres[0:T, g * NB + b, :]

            def xn_of(b):
                return xn[0:T, b, :]

            def evict(a, place, g, b, name):
                if a.owners[name] != "dve":
                    return
                bank = fill(a, place, b, name)[1]
                filled(dve, a, place, g, b, name)
                if name == "x":
                    sa, sb_ = ps[0:DA, bank, 0:T], ps[0:DB, bank, 128:128 + T]
                    if a.index == 1:
                        V.tensor_scalar(xTa[:, 0:T], sa, column(LN_A), column(LN_A + 1), ALU.mult, ALU.add)
                        last = V.tensor_scalar(xTb[:, 0:T], sb_, column(LN_B, 1, DB), column(LN_B + 1, 1, DB),
                                               ALU.mult, ALU.add)
                    else:
                        V.tensor_copy(xTa[:, 0:T], sa)
                        last = V.tensor_copy(xTb[:, 0:T], sb_)
                elif name == "ra":
                    last = V.tensor_scalar(rTa, ps[0:DA, bank, 0:GT], column(LN_A + 2), column(LN_A + 3),
                                           ALU.mult, ALU.add)
                elif name == "lg":
                    last = V.tensor_copy(table(1), ps[0:T, bank, 0:NB * E])
                elif name == "ct":
                    V.tensor_copy(table(5)[:, 0:E], run[0:T, :])
                    last = V.tensor_copy(route[0:T, 9 * NB * E:11 * NB * E], ps[0:T, bank, 0:2 * NB * E])
                elif name[0] == "k":
                    tiles = tiles_of(a, name)
                    if a.index == 0:
                        n, t0 = len(tiles), tiles[0]
                        last = V.tensor_tensor(KT[:, t0:t0 + n, :],
                                               ps[:, bank, 0:n * T].rearrange("p (m t) -> p m t", m=n),
                                               column(BK + t0, n).unsqueeze(2).to_broadcast([128, n, T]), ALU.add)
                    else:
                        for j, tile in enumerate(tiles):
                            w = a.tiles[tile]
                            last = V.tensor_scalar(KT[0:w, tile, :], ps[0:w, bank, j * T:(j + 1) * T],
                                                   float(a.hd) ** -0.5, column(ANC + tile, 1, w),
                                                   ALU.mult, ALU.add)
                else:
                    n = a.heads // a.halves
                    half, w = int(name[1]), n * a.hd
                    src = ps[0:T, bank, 0:w].rearrange("p (h x) -> p h x", h=n)
                    dst = vview(a)[:, half * n:(half + 1) * n, 0:a.hd]
                    c = 2 * D + half * w
                    last = V.tensor_tensor(dst, src, rows[0:T, c:c + w].rearrange("p (h x) -> p h x", h=n),
                                           ALU.add)
                last.then_inc(s_xd, 1)

            def less_max(a, g, s):
                step = (a.index * GROUPS + g) * UNITS
                n = a.n[s % 2]
                dve.wait_ge(s_s, step + s + 1)
                m = mx[0:T, s % 2, 0:2 * n].rearrange("p (k i) -> p k i", k=2)
                wait(dve, s_sub, step + s - 1)
                ch.after(V.tensor_reduce(m, scores_view(a, s), AX.X, ALU.max))
                wait(dve, s_pt, step + s - 1)
                V.tensor_tensor(probs(a, s), scores_view(a, s),
                                m.unsqueeze(3).to_broadcast([T, 2, n, T]), ALU.subtract).then_inc(s_sub, 1)

            def clip_body(a, place, g, b, more):
                step = (a.index * GROUPS + g) * UNITS
                clip = (a.index * GROUPS + g) * NB
                s = 2 * b
                ahead = place != "last"
                routing = a.index == 1 and place != "first"

                def evictions(slot):
                    for name in a.slots[slot] if more else []:
                        evict(a, place, g, b, name)

                def heads_normalized(s):
                    n = a.n[s % 2]
                    dve.wait_ge(s_o, step + s + 1)
                    o = heads_out(a, s)
                    r = rsum[0:T, s % 2, 0:2 * n].rearrange("p (k i) -> p k i", k=2)
                    wait(dve, s_on, step + s - 1)
                    ch.after(V.reciprocal(r, o[:, :, :, a.hd]))
                    wait(dve, s_ot, clip + b)
                    V.tensor_tensor(a.osb_view(osb, s % 2), o[:, :, :, 0:a.hd],
                                    r.unsqueeze(3).to_broadcast([T, 2, n, a.hd]), ALU.mult).then_inc(s_on, 1)

                if routing and b == 3:
                    evict(a, place, g, 2, "lg")
                if more:
                    evict(a, place, g, b, "x")
                less_max(a, g, s + 1)
                evictions(0)
                if ahead:
                    if a.index == 0 and b == 2:
                        apply(norm(a, place, g, "next"), hid_of(g + 1), xn_of)
                    if a.index == 1 and b == 2:
                        n = norm(a, place, g, "next")
                        measure(n, xres_of(g + 1))
                    if a.index == 2 and b == 0:
                        gather_rows(g + 1)
                if routing:
                    if b == 1:
                        dve.wait_ge(s_hup, (GROUPS + routed_group(place, g) + 1) * NB)
                        measure(norm(a, place, g, "route"), xres_of(routed_group(place, g)))
                    if b == 3:
                        took(dve, a, place, g, 2, "lg")
                        one_hots(routed_group(place, g))
                heads_normalized(s)
                evictions(1)
                if ahead:
                    if a.index == 0 and b == 1:
                        measure(norm(a, place, g, "next"), hid_of(g + 1))
                    if a.index == 1 and b == 0:
                        measure(norm(a, place, g, "own"), hid_of(g + 1))
                    if a.index and b == 2:
                        n = norm(a, place, g, "next")
                        apply(n, xres_of(g + 1) if a.index == 1 else hid_of(g + 1), xn_of)
                evictions(2)
                if routing and b == 2:
                    evict(a, place, g, b, "ra")
                heads_normalized(s + 1)
                if more:
                    less_max(a, g, s + 2)
                evictions(3)
                evictions(4)
                dve.wait_ge(s_y, clip + b + 1)
                if a.index == 0:
                    dve.wait_ge(s_res, g + 1)
                dst = xres[0:T, g * NB + b, :] if a.index == 1 else hid[0:T, g * NB + b, :]
                V.tensor_tensor(dst, ps[0:T, 7, 0:D], dst, ALU.add).then_inc(s_hup, 1)
                if a.index == 1 and ahead and b == 0:
                    n = norm(a, place, g, "own")
                    apply(n, hid_of(g + 1), xres_of(g + 1))
                if a.index == 2 and ahead and b == 1:
                    mix(g + 1)
                    measure(norm(a, place, g, "next"), hid_of(g + 1))
                if routing and b == 1:
                    for k in range(2 * NB):
                        wait(dve, s_scat[k], 16 * routed_group(place, g))
                    apply(norm(a, place, g, "route"), xres_of(routed_group(place, g)), xrow_of)
                if routing and b == 3:
                    evict(a, place, g, 3, "ct")
                    took(dve, a, place, g, 3, "ct")
                    rows_found(routed_group(place, g))

            def xrow_of(b):
                return xrow[0:T, b, :]

            def table(k, n=NB * E):
                return route[0:T, k * NB * E:k * NB * E + n]

            def per_expert(x):
                return x.rearrange("p (b e) -> p b e", b=NB)

            first, other = table(7), table(8)
            number = rstd2[0:T, 0:NB]

            def one_hots(g):
                logits = table(1)
                rev = const("rev", T)
                best = kept[0:T, 0:NB]
                second = kept[0:T, NB:2 * NB]

                def one_hot(values, top, dst):
                    ch.after(V.tensor_reduce(top, per_expert(values), AX.X, ALU.max))
                    ch.after(V.tensor_tensor(per_expert(table(2)), per_expert(values),
                                             top.unsqueeze(2).to_broadcast([T, NB, E]), ALU.is_equal))
                    ch.after(V.tensor_tensor(table(2), table(2), rev, ALU.mult))
                    ch.after(V.tensor_reduce(number, per_expert(table(2)), AX.X, ALU.max))
                    ch.after(V.tensor_tensor(per_expert(dst), per_expert(rev),
                                             number.unsqueeze(2).to_broadcast([T, NB, E]), ALU.is_equal))

                one_hot(logits, best, first)
                ch.after(V.scalar_tensor_tensor(table(3), first, -3.0e38, logits, ALU.mult, ALU.add))
                one_hot(table(3), second, other)
                V.tensor_copy(hot[0:T, 0, bass.ds(g * NB, NB), :], per_expert(first))
                V.tensor_copy(hot[0:T, 1, bass.ds(g * NB, NB), :], per_expert(other))
                V.tensor_tensor(gap[0:T, bass.ds(g * NB, NB)], second, best, ALU.subtract)
                V.tensor_tensor(table(0), first, other, ALU.add).then_inc(s_hot, 1)

            def rows_found(g):
                before, totals, base = table(9), per_expert(table(10)), per_expert(table(5))
                for b in range(1, NB):
                    ch.after(V.tensor_tensor(base[:, b, :], base[:, b - 1, :], totals[:, b - 1, :], ALU.add))
                ch.after(V.tensor_tensor(run[0:T, :], base[:, NB - 1, :], totals[:, NB - 1, :], ALU.add))
                ch.after(V.tensor_tensor(table(6), table(5), before, ALU.add))
                for k, h in ((0, first), (1, other)):
                    ch.after(V.tensor_tensor(table(2), table(6), h, ALU.mult))
                    ch.after(V.tensor_reduce(number, per_expert(table(2)), AX.X, ALU.add))
                    V.tensor_copy(pos[0:T, k, bass.ds(g * NB, NB)], number)
                    last = V.tensor_copy(idx[0:T, k, :], number)
                    if k == 0:
                        ch.after(last)
                last.then_inc(s_idx, 1)

            def tables():
                P = slice(0, T)
                count, tiles, end, adjust = (tl[P, k, :] for k in range(4))
                ch.after(V.tensor_tensor(count, run[P, :], const("region", T), ALU.subtract))
                ch.after(V.tensor_copy(padrow[0:1, :], run[0:1, :]))
                sp8 = spread[P, :].rearrange("p (e k) -> p e k", e=E)
                ch.after(V.tensor_tensor(sp8, count.unsqueeze(2).to_broadcast([T, E, 32]),
                                         const("bounds", T).rearrange("p (e k) -> p e k", e=E), ALU.is_gt))
                ch.after(V.tensor_reduce(tiles, sp8, AX.X, ALU.add))
                ch.after(V.tensor_copy(end, tiles))
                for e in range(1, E):
                    ch.after(V.tensor_tensor(end[:, e:e + 1], end[:, e:e + 1], end[:, e - 1:e], ALU.add))
                ch.after(V.tensor_tensor(adjust, end, tiles, ALU.subtract))
                start = tiles
                ch.after(V.tensor_copy(start, adjust))
                ch.after(V.scalar_tensor_tensor(adjust, adjust, 128.0, const("region", T), ALU.mult, ALU.subtract))
                n = TILES + LOADED
                shape = [1, n, E]

                def grid(x):
                    return x.rearrange("p (t e) -> p t e", t=n)

                t_ = grid(const("tile", 1))
                mine, work, work2 = (grid(tabf[0:1, k, :]) for k in range(3))
                ch.after(V.tensor_tensor(work, t_, start[0:1, :].unsqueeze(1).to_broadcast(shape), ALU.is_ge))
                ch.after(V.tensor_tensor(work2, t_, end[0:1, :].unsqueeze(1).to_broadcast(shape), ALU.is_lt))
                ch.after(V.tensor_tensor(mine, work, work2, ALU.mult))
                ch.after(V.scalar_tensor_tensor(work, t_, 128.0, adjust[0:1, :].unsqueeze(1).to_broadcast(shape),
                                                ALU.mult, ALU.subtract))
                ch.after(V.tensor_tensor(work, work, mine, ALU.mult))
                ch.after(V.tensor_reduce(work2[:, :, 0], work, AX.X, ALU.add))
                ch.after(V.tensor_copy(tab[0:1, 0, :], work2[:, :, 0]))
                ch.after(V.tensor_tensor(work, grid(const("tile_e", 1)), mine, ALU.mult))
                ch.after(V.tensor_reduce(work2[:, :, 0], work, AX.X, ALU.add))
                V.tensor_copy(tab[0:1, 1, :], work2[:, :, 0]).then_inc(s_tab, 1)
                for k in range(2):
                    big = spread[P, :].rearrange("p (b e) -> p b e", b=CLIPS)
                    ch.after(V.tensor_tensor(big, hot[P, k, :, :],
                                             adjust.unsqueeze(1).to_broadcast([T, CLIPS, E]), ALU.mult))
                    ch.after(V.tensor_reduce(shift[P, :], big, AX.X, ALU.add))
                    ch.after(V.tensor_tensor(pos[P, k, :], pos[P, k, :], shift[P, :], ALU.add))
                dve.wait_ge(s_gexp, 1)
                ch.after(V.tensor_scalar(wgt[P, 0, :], wgt[P, 1, :], 1.0, None, ALU.add))
                ch.after(V.reciprocal(wgt[P, 0, :], wgt[P, 0, :]))
                ch.after(V.tensor_tensor(wgt[P, 1, :], wgt[P, 1, :], wgt[P, 0, :], ALU.mult))

            def mixture():
                def turned(t, par):
                    dve.wait_ge(s_mt, t + 1)
                    V.tensor_scalar(xsT[:, par, 0:128], ps[:, 0, 0:128], column(LN_A + 2), column(LN_A + 3),
                                    ALU.mult, ALU.add)
                    V.tensor_scalar(xsT[0:DB, par, 128:256], ps[0:DB, 0, 128:256], column(LN_B + 2, 1, DB),
                                    column(LN_B + 3, 1, DB), ALU.mult, ALU.add).then_inc(s_mtc, 1)

                def tile(i, par):
                    t = 2 * i + par
                    turned(t + AHEAD, par)
                    dve.wait_ge(s_gt, t + 1)
                    V.tensor_copy(act1T[:, par, :].rearrange("p (k x) -> p k x", k=2),
                                  ps[:, 5:7, 0:384]).then_inc(s_gtc, 1)
                    dve.wait_ge(s_m2p, t + 1)
                    wait(dve, s_st[par], 16 * i)
                    V.tensor_copy(ys[:, par, :], ps[:, 7, 0:D]).then_inc(s_ys, 1)

                turned(0, 0)
                turned(1, 1)
                tile(0, 0)
                tile(0, 1)
                with dve.Fori(1, TILES // 2) as i:
                    tile(i, 0)
                    tile(i, 1)

            def gather_rows(g):
                V.tensor_copy(idy[0:T, :, :], pos[0:T, :, bass.ds(g * NB, NB)]).then_inc(s_idy, 1)

            def mix(g):
                for k in range(2):
                    for b in range(NB):
                        dve.wait_ge(s_got[k * NB + b], 16 * (g + 1))
                        h = hid[0:T, g * NB + b, :]
                        last = V.scalar_tensor_tensor(h, got[0:T, k, b, :], wgt[0:T, k, bass.ds(g * NB + b, 1)],
                                                      h, ALU.mult, ALU.add)
                    if k == 0:
                        ch.after(last)
                ch.after(last)

            for a in LAYERS:
                if a.index == 2:
                    tables()
                    mixture()
                    dve.wait_ge(s_m2p, TILES)
                    dve.wait_ge(s_res, 2 * GROUPS)
                dve.wait_ge(s_hid, GROUPS)
                if a.index:
                    dve.wait_ge(s_hup, a.index * CLIPS)
                V.memset(vview(a)[:, :, a.hd:a.hd + 1], 1.0)
                n = norm(a, "start", 0, "next")
                if a.index == 1:
                    own = norm(a, "start", 0, "own")
                    measure(own, hid_of(0))
                    apply(own, hid_of(0), xres_of(0))
                    measure(n, xres_of(0))
                    apply(n, xres_of(0), xn_of)
                else:
                    if a.index == 2:
                        gather_rows(0)
                        mix(0)
                    measure(n, hid_of(0))
                    apply(n, hid_of(0), xn_of)
                for name in clip_fills(a):
                    evict(a, "start", 0, 0, name)
                less_max(a, 0, 0)
                for b in range(NB):
                    clip_body(a, "first", 0, b, True)
                with dve.Fori(1, GROUPS - 1) as g:
                    ch.enter(g, CHAIN[a.index], 1)
                    for b in range(NB):
                        clip_body(a, "mid", g, b, True)
                    ch.leave(GROUPS - 2)
                for b in range(NB):
                    clip_body(a, "last", GROUPS - 1, b, b < NB - 1)
                if a.index == 1:
                    g = GROUPS - 1
                    dve.wait_ge(s_hup, (GROUPS + g + 1) * NB)
                    measure(norm(a, "tail", g, "route"), xres_of(g))
                    for k in range(2 * NB):
                        dve.wait_ge(s_scat[k], 16 * g)
                    apply(norm(a, "tail", g, "route"), xres_of(g), xrow_of)
                    evict(a, "tail", g, 2, "ra")
                    evict(a, "tail", g, 2, "lg")
                    took(dve, a, "tail", g, 2, "lg")
                    one_hots(g)
                    evict(a, "tail", g, 3, "ct")
                    took(dve, a, "tail", g, 3, "ct")
                    rows_found(g)

            dve.wait_ge(s_hup, 3 * CLIPS)
            dve.wait_ge(s_f2, 48)

            def rows_turned(g):
                dve.wait_ge(s_lx, g + 1)
                V.tensor_copy(xTa[:, :], ps[:, 4, 0:GT])
                ch.after(V.tensor_copy(xTb[:, :], ps[0:DB, 5, 0:GT]))
                V.tensor_copy(clsa[:, :, bass.ds(g * NB, NB)],
                              xTa[:, :].rearrange("p (b t) -> p t b", t=T)[:, 0:NCLS, :]).then_inc(s_lxd, 1)
                V.tensor_copy(clsb[:, :, bass.ds(g * NB, NB)],
                              xTb[:, :].rearrange("p (b t) -> p t b", t=T)[:, 0:NCLS, :]).then_inc(s_cls, 1)

            def last_group(g, more):
                if more:
                    n = NORMS[3] + g + 2
                    measure(n, hid_of(g + 1))
                    dve.wait_ge(s_lx, g + 1)
                    apply(n, hid_of(g + 1), xn_of)
                    rows_turned(g + 1)
                dve.wait_ge(s_res, 2 * GROUPS + g + 1)
                for b in range(NB):
                    dve.wait_ge(s_fy, g * NB + b + 1)
                    V.tensor_tensor(fin[0:T, b, :], ps[0:T, 6 + b % 2, 0:D],
                                    fin[0:T, b, :], ALU.add).then_inc(s_ft, 1)

            measure(NORMS[3] + 1, hid_of(0))
            apply(NORMS[3] + 1, hid_of(0), xn_of)
            rows_turned(0)
            last_group(0, True)
            with dve.Fori(1, GROUPS - 1) as g:
                ch.enter(g, CHAIN[3], 1)
                last_group(g, True)
                ch.leave(GROUPS - 2)
            last_group(GROUPS - 1, False)

            def pairs(c):
                return gate[:, c:c + 12].rearrange("p (i s) -> p i s", s=2)

            def wide(x):
                return x.unsqueeze(2).to_broadcast([CLIPS, NCLS, 2])

            dve.wait_ge(s_cgate, 1)
            logits = ps[0:CLIPS, 4, 0:12].rearrange("p (i s) -> p i s", s=2)
            top, total, least = gate[:, 32:38], gate[:, 40:46], gate[:, 48:54]
            ch.after(V.tensor_reduce(top, logits, AX.X, ALU.max))
            V.tensor_tensor(pairs(0), logits, wide(top), ALU.subtract).then_inc(s_csub, 1)
            dve.wait_ge(s_cge, 1)
            ch.after(V.tensor_reduce(total, pairs(16), AX.X, ALU.add))
            ch.after(V.reciprocal(total, total))
            ch.after(V.tensor_tensor(pairs(16), pairs(16), wide(total), ALU.mult))
            ch.after(V.tensor_reduce(least, pairs(16), AX.X, ALU.min))
            ch.after(V.tensor_tensor(pairs(56), pairs(16), wide(least), ALU.is_gt))
            ch.after(V.tensor_tensor(pairs(16), pairs(16), pairs(56), ALU.mult))
            ch.after(V.tensor_reduce(total, pairs(16), AX.X, ALU.add))
            ch.after(V.tensor_scalar(total, total, 1e-6, None, ALU.max))
            ch.after(V.reciprocal(total, total))
            ch.after(V.tensor_tensor(pairs(16), pairs(16), wide(total), ALU.mult))
            dve.wait_ge(s_clsh, 16 * NCLS)
            for i in range(NCLS):
                dve.wait_ge(s_cy, i + 1)
                for s in range(2):
                    c = (1 + PAIR[i][1 - s]) * D
                    last = V.tensor_tensor(clso[:, i, s, :], ps[0:CLIPS, 6 + i % 2, s * D:(s + 1) * D],
                                           rows2[0:CLIPS, c:c + D], ALU.add)
                last.then_inc(s_ct, 1)
                dve.wait_ge(s_ct, i + 1)
                for s in range(2):
                    last = V.scalar_tensor_tensor(clsh[:, i, :], clso[:, i, s, :],
                                                  gate[:, 16 + 2 * i + s:17 + 2 * i + s],
                                                  clsh[:, i, :], ALU.mult, ALU.add)
                    if s == 0:
                        ch.after(last)
                last.then_inc(s_cfin, 1)

        @block.gpsimd
        def _(pool):
            ch = Chain(pool, s_poolc)
            G = nc.gpsimd
            G.memset(zeros[:, :], 0.0).then_inc(s_setp, 1)
            pool.wait_ge(s_const, 16)
            pool.wait_ge(s_cols, 32)
            pool.wait_ge(s_hid, GROUPS)

            def deviations(count):
                pool.wait_ge(s_var, count)
                ch.after(G.tensor_tensor(rstd[0:T, :], mv[0:T, :, 1], const("eps", T), ALU.add))
                G.tensor_tensor(rstd[0:T, :], rstd[0:T, :], const("half", T), ALU.pow).then_inc(s_rstd, 1)

            def gather(g):
                pool.wait_ge(s_idy, g + 1)
                settled(nc.gpsimd, 0)
                for k in range(2):
                    for b in range(NB):
                        G.indirect_dma_start(
                            out=got[0:T, k, b, :], out_offset=None, in_=expert_out,
                            in_offset=bass.IndirectOffsetOnAxis(ap=idy[0:T, k, b:b + 1], axis=0),
                        ).then_inc(s_got[k * NB + b], 16)

            def add_rows(g, x):
                four = hid[0:T, bass.ds(g * NB, NB), :]
                G.tensor_tensor(four, four, x, ALU.add).then_inc(s_res, 1)

            def with_bias(g, count):
                pool.wait_ge(s_xn, count)
                settled(nc.gpsimd, 1)
                add_rows(g, rows[0:T, D:2 * D].unsqueeze(1).to_broadcast([T, NB, D]))

            def scatter(g):
                pool.wait_ge(s_idx, g + 1)
                settled(nc.gpsimd, 2)
                for k in range(2):
                    for b in range(NB):
                        G.indirect_dma_start(
                            out=routed, in_=xrow[0:T, b, :], in_offset=None,
                            out_offset=bass.IndirectOffsetOnAxis(ap=idx[0:T, k, b:b + 1], axis=0),
                        ).then_inc(s_scat[k * NB + b], 16)

            def group_body(a, place, g):
                if a.index == 0:
                    if place != "last":
                        count = norm(a, place, g, "next")
                        deviations(count)
                        with_bias(g + 1, count)
                elif a.index == 1:
                    if place in ("first", "mid"):
                        deviations(norm(a, place, g, "own"))
                    if place != "first":
                        h = routed_group(place, g)
                        deviations(norm(a, place, g, "route"))
                    if place in ("first", "mid"):
                        deviations(norm(a, place, g, "next"))
                    if place != "first":
                        add_rows(h, xres[0:T, bass.ds(h * NB, NB), :])
                        scatter(h)
                elif place != "last":
                    gather(g + 1)
                    deviations(norm(a, place, g, "next"))

            for a in LAYERS:
                if a.index == 2:
                    for k in range(2):
                        pool.wait_ge(s_st[k], 16 * (TILES // 2))
                    gather(0)
                if a.index == 1:
                    deviations(norm(a, "start", 0, "own"))
                count = norm(a, "start", 0, "next")
                deviations(count)
                if a.index == 0:
                    with_bias(0, count)
                group_body(a, "first", 0)
                with pool.Fori(1, GROUPS - 1) as g:
                    ch.enter(g, CHAIN_POOL[a.index], 1)
                    group_body(a, "mid", g)
                    ch.leave(GROUPS - 2)
                group_body(a, "last", GROUPS - 1)
                if a.index == 1:
                    group_body(a, "tail", GROUPS - 1)
            pool.wait_ge(s_f2, 48)

            def last_rows(g):
                wait(pool, s_out, 16 * g)
                settled(nc.gpsimd, 3)
                G.tensor_tensor(fin[0:T, :, :], hid[0:T, bass.ds(g * NB, NB), :],
                                rows2[0:T, 0:D].unsqueeze(1).to_broadcast([T, NB, D]), ALU.add).then_inc(s_res, 1)

            deviations(NORMS[3] + 1)
            last_rows(0)
            with pool.Fori(1, GROUPS) as g:
                ch.enter(g, CHAIN_POOL[3], 1)
                deviations(NORMS[3] + g + 1)
                last_rows(g)
                ch.leave(GROUPS - 1)

    return nc


def fold(w):
    n = w.shape[1]
    out = np.zeros((128, 2 * n), np.float32)
    out[:, :n] = w[:DA]
    out[:DB, n:] = w[DA:]
    return out


def slots(w, heads, hd, slot):
    if hd == slot:
        return w
    out = np.zeros((w.shape[0], heads, slot), np.float32)
    out[:, :, :hd] = w.reshape(-1, heads, hd)
    return out.reshape(w.shape[0], heads * slot)


def lay_out(x):
    f = {k: np.asarray(v) for k, v in x.items()}
    c = constants()
    d = {"consts": np.concatenate(list(c.values()), 1)}
    clips = f["x"][:, :STEP * T].reshape(CLIPS, T, STEP)[:, :, :FRAME]
    d["frames"] = clips.transpose(2, 0, 1).reshape(FRAME, TOKENS)
    j = np.arange(FRAME)
    window = 0.54 - 0.46 * np.cos(2 * np.pi * j / (FRAME - 1))
    angle = 2 * np.pi * (np.outer(j, np.arange(BINS)) % FRAME) / FRAME
    d["dft"] = (window[:, None] * np.concatenate([np.cos(angle), -np.sin(angle)], 1)).astype(np.float32)
    mel = f["L0_tok_mel_filters"].T
    d["melw"] = np.concatenate([mel, mel], 0)
    d["dct"], d["wproj"] = f["L0_tok_dct"], f["L0_tok_w_proj"]
    bqkv = f["L0_attn_b_qkv"]
    d["rows"] = np.concatenate([f["L0_tok_b_proj"], f["L0_attn_b_out"], bqkv[1536:]])[None]
    cols = np.zeros((128, 42), np.float32)
    cols[:, 0:12] = bqkv[:1536].reshape(12, 128).T
    ln = np.stack([f["L0_ffn_" + k] for k in ("ln1_g", "ln1_b", "ln2_g", "ln2_b")], 1)
    cols[:, 12:16], cols[:DB, 16:20] = ln[:DA], ln[DA:]
    cols[:, 26:34], cols[:DB, 34:42] = f["L0_ffn_Wrouter"][:DA], f["L0_ffn_Wrouter"][DA:]
    d["cols"] = cols
    d["reat"] = f["L0_attn_reattn_weights"].reshape(6, 128, 64).transpose(1, 0, 2).reshape(128, 384)
    anchor = np.zeros((256, 14), np.float32)
    anchor[:D, 0:6] = f["L1_attn_anchor_w"].reshape(D, 6)
    anchor[:D, 6:12] = np.repeat(f["L1_attn_anchors"], 32, 0)
    anchor[:D, 12] = np.repeat(f["L1_attn_lam"], 32)
    d["anchor"] = np.concatenate([anchor[:128], anchor[128:]], 1)
    w = f["L0_attn_w_qkv"]
    d["w0a"], d["w0b"] = w[:DA], w[DA:]
    d["wo0"] = f["L0_attn_w_out"].reshape(6, 128, D).transpose(1, 0, 2).reshape(128, 6 * D)
    w = f["L0_ffn_Wqkv"]
    w = np.concatenate([slots(w[:, :D], 12, 16, 32), slots(w[:, D:2 * D], 12, 16, 32), w[:, 2 * D:]], 1)
    d["w1"] = np.concatenate([fold(w), fold(f["L0_ffn_Wproj"])], 1)
    w = np.concatenate([f["L1_attn_" + k].T for k in ("Wq", "Wk", "Wv")], 1)
    d["w2"] = np.concatenate([fold(w), fold(f["L1_attn_Wo"].T)], 1)
    w = f["L0_ffn_W1"].transpose(1, 0, 2).reshape(D, E * FF)
    d["m1a"], d["m1b"] = w[:DA], w[DA:]
    d["m2"] = f["L0_ffn_W2"].reshape(E, FJ, 128, D).transpose(2, 0, 1, 3).reshape(128, E * FJ * D)
    w = f["L1_ffn_A1_W"].transpose(1, 0, 2).reshape(D, NEXP * FF)
    d["a1"] = fold(w)
    d["f"] = np.concatenate([fold(f["L1_ffn_moe0_W1"]),
                             f["L1_ffn_moe0_W2"].reshape(FJ, 128, D).transpose(1, 0, 2).reshape(128, FJ * D)], 1)
    d["a2"] = f["L1_ffn_A2_W"].reshape(NEXP, FJ, 128, D).transpose(2, 0, 1, 3).reshape(128, NEXP * FJ * D)
    d["rows2"] = np.concatenate([f["L1_ffn_moe0_b2"], f["L1_ffn_A2_b"].reshape(-1)])[None]
    last = np.zeros((128, 80), np.float32)
    last[:, 0:6] = f["L1_ffn_moe0_b1"].reshape(6, 128).T
    last[:, 6:36] = f["L1_ffn_A1_b"].reshape(30, 128).T
    g = f["L1_ffn_G_W"].transpose(1, 0, 2).reshape(D, 2 * NCLS)
    last[:, 40:52], last[:DB, 60:72] = g[:DA], g[DA:]
    d["lastcols"] = last
    return {k: np.ascontiguousarray(v) for k, v in d.items()}


def kernel(**inputs):
    import concourse.bacc as bacc
    from concourse.bass_utils import run_bass_kernel_spmd

    nc = bacc.Bacc("TRN2", target_bir_lowering=False, num_devices=1)
    arrays, aps = {}, {}
    for name, a in lay_out(inputs).items():
        arrays[f"in_{name}"] = a
        aps[name] = nc.dram_tensor(f"in_{name}", a.shape, mybir.dt.from_np(a.dtype), kind="ExternalInput").ap()
    out = nc.dram_tensor("out", (CLIPS, T, D), F32, kind="ExternalOutput").ap()
    build(nc, aps, out)
    r = run_bass_kernel_spmd(nc, [arrays], core_ids=[0])
    return r.results[0]["out"]
```

```python
from contextlib import ExitStack

import numpy as np

import concourse.bass as bass
from concourse import mybir

F32 = mybir.dt.float32
I32 = mybir.dt.int32
U32 = mybir.dt.uint32
ALU = mybir.AluOpType
ACT = mybir.ActivationFunctionType
AX = mybir.AxisListType

CLIPS, SAMPLES = 32, 20000
FRAME, STEP = 100, 160
T = 1 + (SAMPLES - FRAME) // STEP
BINS = FRAME // 2 + 1
MELS, MFCC = 40, 13
D = 192
DA, DB = 128, D - 128
NB = 4
UNIT = 3
GROUPS = CLIPS // NB
GT = NB * T
FF = 768
FJ = FF // 128
E = 8
TOKENS = CLIPS * T
REGION = TOKENS + 128
TILES = (2 * TOKENS - E) // 128 + E
AHEAD = 2
LOADED = 2 * AHEAD
EPS_LN = 1e-5
NCLS = 6
NEXP = 5
PAIR = [(0, 3), (0, 4), (1, 3), (1, 4), (2, 3), (2, 4)]
SERVES = [[i for i in range(NCLS) if e in PAIR[i]] for e in range(NEXP)]


class Attn:

    def __init__(self, index, heads, hd, slot, owners, slots):
        self.index, self.heads, self.hd, self.slot = index, heads, hd, slot
        self.rg = min(128 // slot, heads // UNIT)
        self.tiles = [self.rg * slot] * (heads // self.rg)
        self.qk = sum(self.tiles)
        self.inner = heads * hd
        self.halves = 2 if self.inner > 512 else 1
        self.per_clip = heads // UNIT
        self.units = self.per_clip * NB
        self.owners = owners
        self.slots = slots
        placed = [(b, n) for b in range(NB) for at in slots for n in slots[at]]
        start = [(0, n) for at in slots for n in slots[at]]
        body, first = list(placed), list(placed)
        last = [x for x in placed if x[0] < NB - 1]
        tail = []
        if index == 1:
            def routed(body):
                body = list(body)
                at = body.index((1, "v"))
                body[at:at + 1] = [(1, "v"), (1, "ra"), (1, "rb")]
                body.insert(body.index((2, "x")) + 1, (2, "lg"))
                body.insert(body.index((3, "v")) if (3, "v") in body else len(body), (3, "ct"))
                return body
            body, last = routed(body), routed(last)
            tail = [(1, "ra"), (1, "rb"), (2, "lg"), (3, "ct")]
        self.order = {"start": start, "first": first, "mid": body, "last": last, "tail": tail}
        assert len(body) % 2 == 0
        self.unit0 = 0
        self.before = (0, 0, 0)

    def count(self, fills):
        own = [self.owners[n] for _, n in fills]
        return np.array([len(own), own.count("dve"), own.count("act")])

    def base(self, place, g):
        o = self.order
        upto = np.array(self.before)
        if place == "start":
            return upto, 0 * upto
        upto = upto + self.count(o["start"])
        if place == "first":
            return upto, 0 * upto
        upto = upto + self.count(o["first"])
        mid = self.count(o["mid"])
        if place == "mid":
            return upto - mid, mid
        upto = upto + mid * (GROUPS - 2)
        if place == "last":
            return upto, 0 * upto
        return upto + self.count(o["last"]), 0 * upto

    def total(self):
        return self.base("tail", 0)[0] + self.count(self.order["tail"])

    def head_at(self, h):
        unit, i = divmod(h, UNIT)
        return UNIT * (unit // self.rg) + i, unit % self.rg * self.slot

    def bank_tile(self, b, tile):
        return tile if self.index == 0 else tile + 3 * (b % 2)


class Chain:

    def __init__(self, eng, sem):
        self.eng, self.sem, self.base, self.n, self.i, self.per = eng, sem, 0, 0, None, 0

    def enter(self, i, per, start=0):
        self.i, self.n, self.per, self.start = i, 0, per, start

    def leave(self, trips):
        assert self.n == self.per, (self.n, self.per)
        self.base, self.i = self.base + trips * self.per, None

    def after(self, ins):
        ins.then_inc(self.sem, 1)
        self.n += 1
        if self.i is None:
            self.base += 1
            self.eng.wait_ge(self.sem, self.base)
        else:
            self.eng.wait_ge(self.sem, self.base - self.start * self.per + self.i * self.per + self.n)


def wait(eng, sem, count):
    if not isinstance(count, (int, np.integer)) or count > 0:
        eng.wait_ge(sem, int(count) if isinstance(count, np.integer) else count)


def layers():
    owners = [
        dict(x="dve", q0="act", k0="dve", q1="act", k1="dve", v0="dve", v1="dve"),
        dict(x="act", q="act", k="act", v="act", ra="dve", rb="act", lg="dve", ct="dve"),
        dict(x="dve", q="act", k="dve", v="act"),
    ]
    slots = [
        {(0, 0): ["x"], (0, 1): ["q0"], (1, 0): ["k0"], (2, 0): ["q1"], (3, 0): ["k1"], (3, 1): ["v0"],
         "turned": ["v1"]},
        {(0, 0): ["x"], (0, 1): ["q"], (1, 0): ["k"], (2, 0): ["v"]},
        {(0, 0): ["x"], (0, 1): ["q"], (1, 0): ["k"], (1, 1): ["v"]},
    ]
    out, before, units = [], np.zeros(3, int), 0
    for i, (heads, hd, slot) in enumerate([(12, 64, 64), (12, 16, 32), (6, 32, 32)]):
        a = Attn(i, heads, hd, slot, owners[i], slots[i])
        a.before, a.unit0 = before, units
        before, units = a.total(), units + a.units * GROUPS
        out.append(a)
    return out


LAYERS = layers()
WARM = [[], [1, 1, 2, 3], [0, 0, 1, 1]]
CHAIN = [33, 56, 19, 2]
CHAIN_POOL = [2, 6, 2, 1]


def constants():
    c = {}
    c["ident"] = np.eye(128)
    c["before"] = np.triu(np.ones((128, 128)), 1)
    c["ones"] = np.ones((128, 128))
    e = np.arange(E)
    c["rev"] = np.tile(E - e, (128, NB))
    c["region"] = np.tile(e * REGION, (128, 1))
    c["bounds"] = np.tile(np.tile(128 * np.arange(32), E), (128, 1))
    t = np.arange(TILES + LOADED)
    c["tile"] = np.tile(np.repeat(t, E), (128, 1))
    c["tile_e"] = np.tile(np.tile(e, TILES + LOADED), (128, 1))
    c["pair"] = np.kron(np.eye(2), np.ones((64, 64)))
    c["tiny"] = np.full((128, 1), 1e-6)
    c["eps"] = np.full((128, NB), EPS_LN)
    c["half"] = np.full((128, 4), -0.5)
    return {k: np.asarray(v, np.float32) for k, v in c.items()}


def const_columns():
    at, out = 0, {}
    for k, v in constants().items():
        out[k] = (at, v.shape[1])
        at += v.shape[1]
    return out, at


def build(nc, A, out):
    cols, ncols = const_columns()
    with ExitStack() as ctx:
        def sb(name, shape, dt=F32):
            return ctx.enter_context(nc.sbuf_tensor(name, shape, dt))

        def sem(name):
            return ctx.enter_context(nc.semaphore(name))

        routed = nc.dram_tensor("routed_rows", (E * REGION, D), F32).ap()
        expert_out = nc.dram_tensor("expert_rows", (TILES * 128, D), F32).ap()

        cst = sb("cst", [128, ncols])
        hid = sb("hid", [128, CLIPS, D])
        rows = sb("rows", [128, 2 * D + 768])
        region1 = sb("region1", [128, 2 * E * FF])
        region2 = sb("region2", [128, E * FJ * D])
        region3 = sb("region3", [128, 13712])
        xn = sb("xn", [128, NB, D])
        xTa = sb("xTa", [DA, GT])
        xTb = sb("xTb", [DB, GT])
        w_l1 = sb("w_l1", [128, 2 * 960 + 2 * D])
        colsm = sb("colsm", [128, 64])
        stats = sb("stats", [128, NB, 6])
        mv3 = sb("mv3", [128, 3, NB, 2])
        rstd3 = sb("rstd3", [128, 3, NB])
        mx = sb("mx", [128, 2, 6])
        rsum = sb("rsum", [128, 2, 6])
        smallw = sb("smallw", [128, 640])
        route = sb("route", [128, 12 * NB * E])
        hot = sb("hot", [128, 2, CLIPS, E])
        gap = sb("gap", [128, CLIPS])
        pos = sb("pos", [128, 2, CLIPS])
        wgt = sb("wgt", [128, 2, CLIPS])
        run = sb("run", [128, E])
        spread = sb("spread", [128, E * 32])
        tl = sb("tl", [128, 4, E])
        tab = sb("tab", [1, 2, TILES + LOADED], I32)
        padrow = sb("padrow", [1, E], I32)
        idx = sb("idx", [128, 2, NB], U32)
        idy = sb("idy", [128, 2, NB], U32)
        zeros = sb("zeros", [128, D])
        rstd2 = sb("rstd2", [128, NB])
        kept = sb("kept", [128, 2 * NB])
        nudge = sb("nudge", [1, 8])
        shift = sb("shift", [128, CLIPS])

        ps = ctx.enter_context(nc.psum_tensor("ps", [128, 8, 512], F32))

        def const(name, p=128):
            a, n = cols[name]
            return cst[0:p, a:a + n]

        ident = const("ident")

        w0a = region2[:, 0:2304]
        w0b = region2[0:DB, 2304:4608]
        wo0 = region2[:, 4608:5760].rearrange("p (j n) -> p j n", j=6)
        QT = region3[:, 0:750].rearrange("p (m t) -> p m t", t=T)
        KT = region3[:, 750:1500].rearrange("p (m t) -> p m t", t=T)
        Vr = region3[:, 1500:2280]
        Pr = region3[:, 2280:3030].rearrange("p (b x) -> p b x", b=2)
        PTr = region3[:, 3780:4530].rearrange("p (b x) -> p b x", b=2)
        osb = region3[:, 5280:6048]
        OT = region3[:, 6048:6798].rearrange("p (j t) -> p j t", t=T)
        rTa = region3[:, 3030:3030 + GT]
        rTb = region3[0:DB, 5480:5480 + GT]
        xres = region3[:, 6800:6800 + CLIPS * D].rearrange("p (b d) -> p b d", b=CLIPS)
        xrow = region3[:, 12944:12944 + NB * D].rearrange("p (b d) -> p b d", b=NB)
        w_l2 = region3[:, 6800:6800 + 1536]
        got = region3[:, 8400:8400 + 8 * D].rearrange("p (s b d) -> p s b d", s=2, b=NB)
        tabf = region3[0:1, 10000:10000 + 3 * (TILES + LOADED) * E].rearrange("p (k x) -> p k x", k=3)
        LW = [
            (w0a, w0b, [wo0[:, j, :] for j in range(6)]),
            (w_l1[:, 0:960], w_l1[0:DB, 960:1920], [w_l1[:, 1920:2112], w_l1[0:DB, 2112:2304]]),
            (w_l2[:, 0:576], w_l2[0:DB, 576:1152], [w_l2[:, 1152:1344], w_l2[0:DB, 1344:1536]]),
        ]
        frames = region3[0:FRAME, 0:TOKENS]
        spectrum = region3[0:2 * BINS, 5000:5000 + GT]
        power = region3[0:2 * BINS, 4000:4000 + GT]
        logmel = region3[0:MELS, 4500:4500 + GT]
        melw = smallw[0:2 * BINS, 0:MELS]
        dct = smallw[0:MFCC, 40:80]
        wproj = smallw[0:MFCC, 80:272]
        combined = smallw[0:MELS, 272:464]
        dft = smallw[0:FRAME, 464:464 + 2 * BINS]
        M0 = 0
        xs = region3[:, M0:M0 + 384].rearrange("p (b d) -> p b d", b=2)
        xsT = region3[:, M0 + 384:M0 + 896].rearrange("p (b x) -> p b x", b=2)
        act1 = region3[:, M0 + 896:M0 + 2432].rearrange("p (b x) -> p b x", b=2)
        act1T = region3[:, M0 + 2432:M0 + 3968].rearrange("p (b x) -> p b x", b=2)
        ys = region3[:, M0 + 3968:M0 + 4352].rearrange("p (b d) -> p b d", b=2)
        m1a = region1[:, 0:E * FF]
        m1b = region1[0:DB, E * FF:2 * E * FF]
        m2 = region2[:, :]
        a1a = region1[:, 0:NEXP * FF]
        a1b = region1[0:DB, NEXP * FF:2 * NEXP * FF]
        f1a = region1[:, 7680:7680 + FF]
        f1b = region1[0:DB, 7680 + FF:7680 + 2 * FF]
        f2 = region1[:, 9216:9216 + FJ * D]
        a2 = region2[:, 0:NEXP * FJ * D]
        rows2 = region2[:, 5760:5760 + (1 + NEXP) * D]
        actF = region3[:, 0:6 * GT].rearrange("p (j t) -> p j t", j=FJ)
        fin = region3[:, 3000:3000 + NB * D].rearrange("p (b d) -> p b d", b=NB)
        clsa = region3[:, 3800:3800 + NCLS * CLIPS].rearrange("p (i b) -> p i b", i=NCLS)
        clsb = region3[0:DB, 4000:4000 + NCLS * CLIPS].rearrange("p (i b) -> p i b", i=NCLS)
        clsh = region3[0:CLIPS, 4200:4200 + NCLS * D].rearrange("p (i d) -> p i d", i=NCLS)
        clsact = region3[:, 5400:5400 + NEXP * FJ * 96].rearrange("p (e j x) -> p e j x", e=NEXP, j=FJ)
        clso = region3[0:CLIPS, 8300:8300 + 2 * NCLS * D].rearrange("p (i s d) -> p i s d", i=NCLS, s=2)
        gate = region3[0:CLIPS, 10700:10800]
        b1c = region3[:, 10800:10806]
        a1bc = region3[:, 10806:10836]
        gwa = region3[:, 10840:10852]
        gwb = region3[0:DB, 10860:10872]

        def column(a, n=1, p=128):
            return colsm[0:p, a:a + n]

        BQ, BK, LN_A, LN_B, HSC, ROUT_A, ROUT_B, ANC = 0, 6, 12, 16, 20, 26, 34, 42

        s_const = sem("consts_loaded")
        s_tokw = sem("token_weights_loaded")
        s_frames = sem("frames_loaded")
        s_w0 = sem("layer0_weights_loaded")
        s_cols = sem("columns_loaded")
        s_w1 = sem("layer1_weights_loaded")
        s_w2 = sem("layer2_weights_loaded")
        s_m1 = sem("mixture_w1_loaded")
        s_m2 = sem("mixture_w2_loaded")
        s_f1 = sem("last_w1_loaded")
        s_f2 = sem("last_w2_loaded")
        s_reat = sem("head_weights_loaded")
        s_anc = sem("anchors_loaded")
        s_set = sem("setup_done_by_vector")
        s_setp = sem("zero_rows_ready")
        s_comb = sem("mfcc_projection_in_psum")
        s_hsum = sem("head_sums_in_psum")
        s_dft = sem("spectrum_in_psum")
        s_pow = sem("power_in_sbuf")
        s_mel = sem("mel_in_psum")
        s_log = sem("logmel_in_sbuf")
        s_tok = sem("tokens_in_psum")
        s_hid = sem("tokens_in_hid")
        s_dve = sem("vector_chain")
        s_poolc = sem("pool_chain")
        s_var = sem("variances_ready")
        s_xn = sem("normalized_rows_ready")
        s_rstd = sem("reciprocal_deviations_ready")
        s_res = sem("bias_added_to_residual")
        s_x = sem("projection_bank_full")
        s_xd = sem("projection_taken_by_vector")
        s_xc = sem("projection_taken_by_scalar")
        s_s = sem("scores_in_psum")
        s_sub = sem("scores_less_max")
        s_exp = sem("probs_ready")
        s_pt = sem("probs_transposed_in_psum")
        s_ptc = sem("probs_transposed_in_sbuf")
        s_o = sem("heads_out_in_psum")
        s_on = sem("heads_out_normalized")
        s_ot = sem("heads_out_transposed_in_psum")
        s_otc = sem("heads_out_transposed_in_sbuf")
        s_y = sem("attention_out_in_psum")
        s_hup = sem("attention_out_taken")
        s_hot = sem("one_hots_ready")
        s_idx = sem("scatter_rows_ready")
        s_scat = [sem(f"rows_scattered_{k}") for k in range(2 * NB)]
        s_tab = sem("tile_tables_ready")
        s_padrow = sem("pad_rows_known")
        s_pad = sem("pad_rows_written")
        s_gexp = sem("gap_exponential_ready")
        s_ld = [sem(f"tile_loaded_{k}") for k in range(2)]
        s_mt = sem("tile_transposed_in_psum")
        s_mtc = sem("tile_transposed_in_sbuf")
        s_m1p = sem("expert_hidden_in_psum")
        s_gel = sem("expert_gelu_ready")
        s_gt = sem("expert_gelu_transposed_in_psum")
        s_gtc = sem("expert_gelu_transposed_in_sbuf")
        s_m2p = sem("expert_out_in_psum")
        s_ys = sem("expert_out_in_sbuf")
        s_st = [sem(f"tile_stored_{k}") for k in range(2)]
        s_idy = sem("gather_rows_ready")
        s_got = [sem(f"expert_rows_gathered_{k}") for k in range(2 * NB)]
        s_fh = sem("last_hidden_in_psum")
        s_fg = sem("last_gelu_ready")
        s_fy = sem("last_out_in_psum")
        s_ft = sem("last_out_taken")
        s_lx = sem("last_rows_transposed_in_psum")
        s_lxd = sem("last_rows_taken_by_vector")
        s_out = sem("output_stored")
        s_clsh = sem("class_rows_moved")
        s_cls = sem("class_columns_kept")
        s_ch = sem("class_hidden_in_psum")
        s_cg = sem("class_gelu_ready")
        s_cgate = sem("class_gates_in_psum")
        s_cge = sem("class_gate_exponentials")
        s_csub = sem("class_gate_less_max")
        s_cy = sem("class_out_in_psum")
        s_ct = sem("class_out_taken")
        s_cfin = sem("class_rows_ready")
        s_cout = sem("class_rows_stored")

        block = ctx.enter_context(nc.Block())

        def settled(eng, place=0):
            if eng is nc.vector:
                return nc.vector.memset(nudge[0:1, 0:1], 0.0)
            return nc.gpsimd.tensor_tensor(nudge[0:1, 1 + place:2 + place], const("half", 1)[:, 0:1], const("half", 1)[:, 0:1], ALU.add)

        def fill(a, place, b, name):
            k = a.order[place].index((b, name))
            return k, 2 + int(a.base(place, 0)[0][0] + k) % 2

        def filled(eng, a, place, g, b, name):
            base, per = a.base(place, g)
            eng.wait_ge(s_x, int(base[0]) + fill(a, place, b, name)[0] + 1 + (int(per[0]) * g if per[0] else 0))

        def add_up(n, per, g):
            return n + (per * g if per else 0)

        def taken_upto(eng, a, place, g, k, who):
            base, per = a.base(place, g)
            n = int(base[who])
            if k >= 0:
                n += int(a.count(a.order[place][:k + 1])[who])
            elif k == -2 and place in ("first", "mid", "last"):
                n -= int(a.count(a.order["start"][-1:])[who])
            wait(eng, (None, s_xd, s_xc)[who], add_up(n, int(per[who]), g))

        def who_takes(a, name):
            return 1 if a.owners[name] == "dve" else 2

        def bank_free(eng, a, place, g, b, name):
            k = fill(a, place, b, name)[0] - 2
            if k >= 0:
                took(eng, a, place, g, *a.order[place][k])
            else:
                for who in (1, 2):
                    taken_upto(eng, a, place, g, k, who)

        def took(eng, a, place, g, b, name):
            taken_upto(eng, a, place, g, fill(a, place, b, name)[0], who_takes(a, name))

        def took_for(eng, a, place, g, b, name):
            if b > 0:
                took(eng, a, place, g, b - 1, name)
            elif place == "first":
                took(eng, a, "start", 0, 0, name)
            else:
                order = [n for _, n in a.order["start"]]
                after = order[order.index(name) + 1:]
                assert [n for _, n in a.order["mid"][-1 - len(after):]] == [name] + after
                who = who_takes(a, name)
                base, per = a.base(place, g)
                n = int(base[who]) - int(a.count([(0, n) for n in after])[who])
                wait(eng, (None, s_xd, s_xc)[who], add_up(n, int(per[who]), g))


        NORMS = [0, GROUPS, 4 * GROUPS, 5 * GROUPS]

        def norm(a, place, g, which):
            n = NORMS[a.index]
            if a.index != 1:
                return n + (1 if place == "start" else g + 2)
            if place == "start":
                return n + dict(own=1, next=2)[which]
            if place == "first":
                return n + dict(own=3, next=4)[which]
            if place == "mid":
                return n + 3 * g + dict(route=2, own=3, next=4)[which]
            return n + 3 * (GROUPS - 1) + (2 if place == "last" else 3)

        def norm_of(a, place, g):
            if place == "start" or place == "first":
                return norm(a, "start", 0, "next")
            if a.index != 1:
                return NORMS[a.index] + g + 1
            return NORMS[1] + 3 * g + 1

        def routed_group(place, g):
            return GROUPS - 1 if place == "tail" else g - 1

        def vview(a, b):
            n = a.heads * (a.hd + 1)
            at = 0 if a.index == 0 else n * (b % 2)
            return Vr[0:T, at:at + n].rearrange("p (h x) -> p h x", h=a.heads)

        def steps(a, g):
            return a.unit0 + g * a.units

        def three(x):
            return x.rearrange("p (i t) -> p i t", i=UNIT)

        def scores_view(s):
            return three(ps[0:T, s % 2, 0:UNIT * T])

        def probs(s):
            return Pr[0:T, s % 2, 0:UNIT * T]

        def probsT(s):
            return PTr[0:T, s % 2, 0:UNIT * T]

        def heads_out(a):
            return three(ps[0:T, 6, 0:UNIT * (a.hd + 1)])

        def unit_heads(a, s):
            return [UNIT * (s % a.per_clip) + i for i in range(UNIT)]

        def heads_turned(a, j, w):
            if a.index == 0:
                return ps[0:w, 4 + j // 3, (j % 3) * T:(j % 3 + 1) * T]
            return ps[0:w, 7, 200 + j * T:200 + (j + 1) * T]

        def out_runs(a):
            return [(c, min(128, a.inner - c)) for c in range(0, a.inner, 128)]

        def tiles_of(a, name):
            if a.halves == 2:
                return range(3 * int(name[1]), 3 * int(name[1]) + 3)
            return range(len(a.tiles))

        def fills_at(a, b, at):
            if a.index == 1 and b == NB - 1 and at in ((2, 0), (3, 1)):
                return ["v"] if at == (3, 1) else []
            return a.slots.get(at, [])

        def later(a, b):
            return a.index > 0 and b < NB - 1

        def following(b):
            return (b + 1) // NB, (b + 1) % NB


        @block.sync
        def _(sp):
            sp.dma_start(cst[:, :], A["consts"]).then_inc(s_const, 16)
            sp.dma_start(melw, A["melw"]).then_inc(s_tokw, 16)
            sp.dma_start(dct, A["dct"]).then_inc(s_tokw, 16)
            sp.dma_start(wproj, A["wproj"]).then_inc(s_tokw, 16)
            sp.dma_start(dft, A["dft"]).then_inc(s_tokw, 16)
            sp.dma_start(frames, A["frames"]).then_inc(s_frames, 16)
            sp.dma_start(rows[:, :], A["rows"].partition_broadcast(128)).then_inc(s_cols, 16)
            sp.dma_start(colsm[:, 0:42], A["cols"]).then_inc(s_cols, 16)
            sp.dma_start(region1[:, 0:384], A["reat"]).then_inc(s_reat, 16)
            sp.dma_start(region1[0:64, 384:384 + 39], A["anchor"]).then_inc(s_anc, 16)
            sp.dma_start(w0a, A["w0a"]).then_inc(s_w0, 16)
            sp.dma_start(w0b, A["w0b"]).then_inc(s_w0, 16)
            sp.dma_start(region2[:, 4608:5760], A["wo0"]).then_inc(s_w0, 16)
            sp.dma_start(w_l1[:, :], A["w1"]).then_inc(s_w1, 16)
            sp.wait_ge(s_set, 1)
            sp.dma_start(m1a, A["m1a"]).then_inc(s_m1, 16)
            sp.dma_start(m1b, A["m1b"]).then_inc(s_m1, 16)
            sp.wait_ge(s_hup, CLIPS)
            sp.dma_start(m2, A["m2"]).then_inc(s_m2, 16)
            sp.wait_ge(s_padrow, 1)
            sp.wait_ge(s_setp, 1)
            for e in range(E):
                r = sp.value_load(padrow[0:1, e:e + 1], min_val=0, max_val=E * REGION - 128)
                sp.dma_start(routed[bass.ds(r, 128), :], zeros[:, :]).then_inc(s_pad, 16)
            sp.wait_ge(s_pad, 16 * E)
            sp.wait_ge(s_tab, 1)
            for k in range(2 * NB):
                sp.wait_ge(s_scat[k], 16 * GROUPS)

            def load_tile(t, par):
                r = sp.value_load(tab[0:1, 0, bass.ds(t, 1)], min_val=0, max_val=E * REGION - 128)
                sp.dma_start(xs[:, par, :], routed[bass.ds(r, 128), :]).then_inc(s_ld[par], 16)

            load_tile(0, 0)
            load_tile(1, 1)
            for par in range(2):
                sp.wait_ge(s_mt, par + 1)
                load_tile(AHEAD + par, par)
            sp.wait_ge(s_res, 2 * GROUPS)
            sp.dma_start(w_l2, A["w2"]).then_inc(s_w2, 16)
            with sp.Fori(0, TILES // 2) as i:
                for par in range(2):
                    sp.wait_ge(s_mt, 2 * i + par + AHEAD + 1)
                    load_tile(2 * i + par + LOADED, par)
                    sp.wait_ge(s_ys, 2 * i + par + 1)
                    sp.dma_start(expert_out[bass.ds((2 * i + par) * 128, 128), :],
                                 ys[:, par, :]).then_inc(s_st[par], 16)
            for par in range(2):
                sp.wait_ge(s_ld[par], 16 * (TILES + LOADED) // 2)

            sp.wait_ge(s_m2p, TILES)
            for k in range(2 * NB):
                sp.wait_ge(s_got[k], 16)
            sp.dma_start(region1[:, 0:7680], A["a1"]).then_inc(s_f1, 16)
            sp.dma_start(region1[:, 7680:7680 + 2 * FF + FJ * D], A["f"]).then_inc(s_f1, 16)
            sp.dma_start(a2, A["a2"]).then_inc(s_f2, 16)
            sp.dma_start(rows2, A["rows2"].partition_broadcast(128)).then_inc(s_f2, 16)
            sp.wait_ge(s_hup, 3 * CLIPS)
            sp.dma_start(region3[:, 10800:10880], A["lastcols"]).then_inc(s_f2, 16)
            for i in range(NCLS):
                sp.dma_start(clsh[:, i, :], hid[i:i + 1, :, :]).then_inc(s_clsh, 16)
            with sp.Fori(0, GROUPS) as g:
                sp.wait_ge(s_ft, NB * (g + 1))
                sp.dma_start(out[bass.ds(g * NB, NB), NCLS:T, :].rearrange("b n d -> n b d"),
                             fin[NCLS:T, :, :]).then_inc(s_out, 16)
            sp.wait_ge(s_cfin, NCLS)
            sp.dma_start(out[:, 0:NCLS, :], clsh).then_inc(s_cout, 16)
            sp.wait_ge(s_out, 16 * GROUPS)
            sp.wait_ge(s_cout, 16)
            for k in range(2):
                sp.wait_ge(s_st[k], 16 * (TILES // 2))

        def mixture_tensor(pe, mm):
            pe.wait_ge(s_m1, 32)
            pe.wait_ge(s_m2, 16)
            pe.wait_ge(s_tab, 1)

            def turn_rows(par, i):
                pe.wait_ge(s_ld[par], 16 * (i + 1))
                nc.tensor.transpose(ps[:, 0, 0:128], xs[:, par, 0:DA], ident)
                nc.tensor.transpose(ps[0:DB, 0, 128:256], xs[:, par, DA:D], ident).then_inc(s_mt, 1)

            def expert_of(t):
                return pe.value_load(tab[0:1, 1, bass.ds(t, 1)], min_val=0, max_val=E - 1)

            def hidden(par, half, e):
                o = ps[:, 1 + 2 * par + half, 0:384]
                mm(o, xsT[:, par, 0:128], m1a[:, bass.ds(e * FF + half * 384, 384)], True, False)
                last = mm(o, xsT[0:DB, par, 128:256], m1b[:, bass.ds(e * FF + half * 384, 384)], False, True)
                if half:
                    last.then_inc(s_m1p, 1)

            def tile(i, par):
                t = 2 * i + par
                e = expert_of(t + 1)
                pe.wait_ge(s_mtc, t + 2)
                wait(pe, s_gel, t)
                hidden(1 - par, 0, e)
                turn_rows(par, i + 1)
                pe.wait_ge(s_gel, t + 1)
                wait(pe, s_gtc, t)
                for j in range(FJ):
                    last = nc.tensor.transpose(ps[:, 5 + j // 3, (j % 3) * 128:(j % 3 + 1) * 128],
                                               act1[:, par, j * 128:(j + 1) * 128], ident)
                last.then_inc(s_gt, 1)
                hidden(1 - par, 1, e)
                e = expert_of(t)
                pe.wait_ge(s_gtc, t + 1)
                wait(pe, s_ys, t)
                for j in range(FJ):
                    last = mm(ps[:, 7, 0:D], act1T[:, par, j * 128:(j + 1) * 128],
                              m2[:, bass.ds(e * (FJ * D) + j * D, D)], j == 0, j == FJ - 1)
                last.then_inc(s_m2p, 1)

            turn_rows(0, 0)
            pe.wait_ge(s_mtc, 1)
            turn_rows(1, 0)
            e = expert_of(0)
            hidden(0, 0, e)
            hidden(0, 1, e)
            tile(0, 0)
            tile(0, 1)
            with pe.Fori(1, TILES // 2) as i:
                tile(i, 0)
                tile(i, 1)

        @block.tensor
        def _(pe):
            def mm(o, lhsT, rhs, first=True, last=True):
                return nc.tensor.matmul(o, lhsT, rhs, start=first, stop=last)

            def keep_warm(n):
                for _ in range(n):
                    mm(ps[:, 7, 0:512], ident, cst[:, 0:512])

            pe.wait_ge(s_const, 16)
            pe.wait_ge(s_tokw, 64)
            mm(ps[0:MELS, 7, 0:D], dct, wproj).then_inc(s_comb, 1)
            pe.wait_ge(s_set, 1)
            mm(ps[:, 6, 0:6], const("pair"), column(HSC, 6)).then_inc(s_hsum, 1)

            pe.wait_ge(s_set, 2)
            pe.wait_ge(s_frames, 16)
            def spectra(g):
                mm(ps[0:2 * BINS, 0, 0:GT], dft, frames[:, bass.ds(g * GT, GT)]).then_inc(s_dft, 1)

            def tokens(g, more):
                pe.wait_ge(s_pow, g + 1)
                mm(ps[0:MELS, 1, 0:GT], melw, power).then_inc(s_mel, 1)
                if more:
                    spectra(g + 1)
                pe.wait_ge(s_log, g + 1)
                wait(pe, s_hid, g)
                for b in range(NB):
                    last = mm(ps[0:T, 2 + b // 2, (b % 2) * D:(b % 2 + 1) * D],
                              logmel[:, b * T:(b + 1) * T], combined)
                last.then_inc(s_tok, 1)

            spectra(0)
            tokens(0, True)
            with pe.Fori(1, GROUPS - 1) as g:
                tokens(g, True)
            tokens(GROUPS - 1, False)

            def project(a, place, g, b, name):
                bank = fill(a, place, b, name)[1]
                wa, wb, _ = LW[a.index]
                if name == "ra":
                    bank_free(pe, a, place, g, b, "rb")
                if name != "rb":
                    bank_free(pe, a, place, g, b, name)
                xa, xb = xTa[:, 0:T], xTb[:, 0:T]
                if name == "x":
                    later, at = (0, 0) if place == "start" else following(b)
                    pe.wait_ge(s_xn, norm(a, place, g, "next") if later else norm_of(a, place, g))
                    nc.tensor.transpose(ps[0:DA, bank, 0:T], xn[0:T, at, 0:DA], ident[0:T, 0:T])
                    last = nc.tensor.transpose(ps[0:DB, bank, 128:128 + T], xn[0:T, at, DA:D], ident[0:T, 0:T])
                elif name[0] in "qk":
                    took(pe, a, place, g, b, "x")
                    for j, tile in enumerate(tiles_of(a, name)):
                        c = a.tiles[0] * tile + (a.qk if name[0] == "k" else 0)
                        w = a.tiles[tile]
                        o = ps[0:w, bank, j * T:(j + 1) * T]
                        mm(o, wa[:, c:c + w], xa, True, False)
                        last = mm(o, wb[:, c:c + w], xb, False, True)
                elif name[0] == "v":
                    w = a.inner // a.halves
                    c = 2 * a.qk + (int(name[1]) * w if a.halves == 2 else 0)
                    o = ps[0:T, bank, 0:w]
                    mm(o, xa, wa[:, c:c + w], True, False)
                    last = mm(o, xb, wb[:, c:c + w], False, True)
                elif name in ("ra", "rb"):
                    if name == "ra":
                        pe.wait_ge(s_xn, norm(a, place, g, "route"))
                    c, w = (0, DA) if name == "ra" else (DA, DB)
                    for i in range(NB):
                        last = nc.tensor.transpose(ps[0:w, bank, i * T:(i + 1) * T],
                                                   xrow[0:T, i, c:c + w], ident[0:T, 0:T])
                elif name == "lg":
                    took(pe, a, place, g, 1, "ra")
                    took(pe, a, place, g, 1, "rb")
                    for i in range(NB):
                        o = ps[0:T, bank, i * E:(i + 1) * E]
                        mm(o, rTa[:, i * T:(i + 1) * T], column(ROUT_A, E), True, False)
                        last = mm(o, rTb[:, i * T:(i + 1) * T], column(ROUT_B, E, DB), False, True)
                else:
                    pe.wait_ge(s_hot, routed_group(place, g) + 1)
                    picked = route[0:T, 0:NB * E]
                    mm(ps[0:T, bank, 0:NB * E], const("before", T)[:, 0:T], picked)
                    last = mm(ps[0:T, bank, NB * E:2 * NB * E], const("ones", T)[:, 0:T], picked)
                last.then_inc(s_x, 1)

            def scores(a, place, g, s):
                b, u = divmod(s, a.per_clip)
                if u == 0 or a.halves == 2 and u == 2:
                    for kind in "qk":
                        name = kind + str(u // 2) if a.halves == 2 else kind
                        if place == "start":
                            took(pe, a, place, g, 0, name)
                        elif a.halves == 2 and u == 2:
                            took_for(pe, a, place, g, b, name)
                        else:
                            took(pe, a, place, g, b - 1, name)
                wait(pe, s_sub, steps(a, g) + s - 1)
                for i, h in enumerate(unit_heads(a, s)):
                    tile, p = a.head_at(h)
                    tile = a.bank_tile(b, tile)
                    last = mm(ps[0:T, s % 2, i * T:(i + 1) * T],
                              QT[p:p + a.slot, tile, :], KT[p:p + a.slot, tile, :])
                last.then_inc(s_s, 1)

            def clip_body(a, place, g, b, more):
                step = steps(a, g)
                clip = (a.index * GROUPS + g) * NB
                U = a.per_clip

                def probs_transposed(s):
                    wait(pe, s_ptc, step + s - 1)
                    if a.index == 0 and s % U < 2:
                        wait(pe, s_otc, clip + b)
                    for _ in range(WARM[a.index].count(s % U)):
                        mm(ps[:, 4 + s % 2, UNIT * T:512], ident, cst[:, 0:512 - UNIT * T])
                    pe.wait_ge(s_exp, step + s + 1)
                    for i in range(UNIT):
                        last = nc.tensor.transpose(ps[0:T, 4 + s % 2, i * T:(i + 1) * T],
                                                   probs(s)[:, i * T:(i + 1) * T], ident[0:T, 0:T])
                    last.then_inc(s_pt, 1)

                def heads(s):
                    pe.wait_ge(s_ptc, step + s + 1)
                    wait(pe, s_on, step + s)
                    if s % U == 0:
                        for name in ("v0", "v1") if a.halves == 2 else ("v",):
                            took_for(pe, a, place, g, b, name)
                    for i, h in enumerate(unit_heads(a, s)):
                        last = mm(heads_out(a)[:, i, :], probsT(s)[:, i * T:(i + 1) * T], vview(a, b)[:, h, :])
                    last.then_inc(s_o, 1)

                def projections(at):
                    for name in fills_at(a, b, at) if more else []:
                        project(a, place, g, b, name)

                def heads_turned_over(b):
                    pe.wait_ge(s_on, step + (b + 1) * U)
                    if a.index == 0:
                        pe.wait_ge(s_ptc, step + (b + 1) * U)
                    wait(pe, s_hup, clip + b)
                    for j, (c, w) in enumerate(out_runs(a)):
                        last = nc.tensor.transpose(heads_turned(a, j, w), osb[0:T, c:c + w], ident[0:T, 0:T])
                    last.then_inc(s_ot, 1)

                def out_projection(b):
                    pe.wait_ge(s_otc, clip + b + 1)
                    for j, (c, w) in enumerate(out_runs(a)):
                        last = mm(ps[0:T, 7, 0:D], OT[0:w, j, :], LW[a.index][2][j], j == 0, c + w == a.inner)
                    last.then_inc(s_y, 1)

                routing = a.index == 1 and place != "first"
                for u in range(U):
                    s = b * U + u
                    probs_transposed(s)
                    if routing and b == 3 and u == 2:
                        project(a, place, g, b, "ct")
                    projections((u, 0))
                    if u == 0 and b and later(a, b - 1):
                        heads_turned_over(b - 1)
                    if u + 2 < U or more and U > 2:
                        scores(a, place, g, s + 2)
                    if u == 0 and b and later(a, b - 1) and U > 2:
                        out_projection(b - 1)
                    heads(s)
                    if u == 0 and b and later(a, b - 1) and U == 2:
                        out_projection(b - 1)
                    if routing and u == U - 1 and b == 1:
                        project(a, place, g, b, "ra")
                        project(a, place, g, b, "rb")
                    if routing and u == 0 and b == 2:
                        project(a, place, g, b, "lg")
                    projections((u, 1))
                if more and U == 2:
                    scores(a, place, g, s + 1)
                if not later(a, b):
                    heads_turned_over(b)
                    projections("turned")
                if more and U == 2:
                    scores(a, place, g, s + 2)
                if not later(a, b):
                    out_projection(b)

            for a, loaded, n in ((LAYERS[0], s_w0, 48), (LAYERS[1], s_w1, 16), (LAYERS[2], s_w2, 16)):
                if a.index == 0:
                    pe.wait_ge(s_set, 3)
                    pe.wait_ge(s_hid, GROUPS)
                if a.index == 2:
                    mixture_tensor(pe, mm)
                    pe.wait_ge(s_gel, TILES)
                    pe.wait_ge(s_gtc, TILES)
                    pe.wait_ge(s_ys, TILES)
                pe.wait_ge(loaded, n)
                for b, name in a.order["start"]:
                    project(a, "start", 0, b, name)
                scores(a, "start", 0, 0)
                scores(a, "start", 0, 1)
                if a.index:
                    pe.wait_ge(s_hup, a.index * CLIPS)
                    keep_warm(6)
                for b in range(NB):
                    clip_body(a, "first", 0, b, True)
                with pe.Fori(1, GROUPS - 1) as g:
                    for b in range(NB):
                        clip_body(a, "mid", g, b, True)
                for b in range(NB):
                    clip_body(a, "last", GROUPS - 1, b, b < NB - 1)
                for b, name in a.order["tail"]:
                    project(a, "tail", GROUPS - 1, b, name)

            pe.wait_ge(s_f1, 32)
            pe.wait_ge(s_f2, 48)
            pe.wait_ge(s_hup, 3 * CLIPS)

            def turned(g):
                pe.wait_ge(s_xn, NORMS[3] + g + 1)
                for k, c, w in ((0, 0, DA), (1, DA, DB)):
                    for b in range(NB):
                        last = nc.tensor.transpose(ps[0:w, 4 + k, b * T:(b + 1) * T],
                                                   xn[0:T, b, c:c + w], ident[0:T, 0:T])
                last.then_inc(s_lx, 1)

            def last_group(g, more):
                pe.wait_ge(s_lxd, g + 1)
                for j in range(FJ):
                    wait(pe, s_fg, g * FJ + j - 1)
                    mm(ps[:, j % 2, 0:GT], f1a[:, j * 128:(j + 1) * 128], xTa[:, :], True, False)
                    mm(ps[:, j % 2, 0:GT], f1b[:, j * 128:(j + 1) * 128], xTb[:, :], False, True).then_inc(s_fh, 1)
                if more:
                    turned(g + 1)
                pe.wait_ge(s_fg, g * FJ + FJ)
                for b in range(NB):
                    wait(pe, s_ft, g * NB + b - 1)
                    for j in range(FJ):
                        last = mm(ps[0:T, 6 + b % 2, 0:D], actF[:, j, b * T:(b + 1) * T],
                                  f2[:, j * D:(j + 1) * D], j == 0, j == FJ - 1)
                    last.then_inc(s_fy, 1)

            turned(0)
            last_group(0, True)
            with pe.Fori(1, GROUPS - 1) as g:
                last_group(g, True)
            last_group(GROUPS - 1, False)

            pe.wait_ge(s_cls, GROUPS)
            for i in range(NCLS):
                mm(ps[0:CLIPS, 4, 2 * i:2 * i + 2], clsa[:, i, :], gwa[:, 2 * i:2 * i + 2], True, False)
                last = mm(ps[0:CLIPS, 4, 2 * i:2 * i + 2], clsb[:, i, :], gwb[:, 2 * i:2 * i + 2], False, True)
            last.then_inc(s_cgate, 1)
            for e in range(NEXP):
                if e >= 2:
                    pe.wait_ge(s_cg, e - 1)
                first, step = SERVES[e][0], SERVES[e][1] - SERVES[e][0]
                n = len(SERVES[e])
                for j in range(FJ):
                    o = ps[:, 2 * (e % 2) + j // 3, (j % 3) * 96:(j % 3) * 96 + n * CLIPS]
                    stop = first + step * (n - 1) + 1
                    c = e * FF + j * 128
                    mm(o, a1a[:, c:c + 128], clsa[:, first:stop:step, :], True, False)
                    last = mm(o, a1b[:, c:c + 128], clsb[:, first:stop:step, :], False, True)
                last.then_inc(s_ch, 1)
            pe.wait_ge(s_cg, NEXP)
            pe.wait_ge(s_ft, CLIPS)
            for i in range(NCLS):
                if i >= 2:
                    pe.wait_ge(s_ct, i - 1)
                for s in range(2):
                    e, f = PAIR[i][s], PAIR[i][1 - s]
                    at = SERVES[e].index(i) * CLIPS
                    for j in range(FJ):
                        c = (f * FJ + j) * D
                        last = mm(ps[0:CLIPS, 6 + i % 2, s * D:(s + 1) * D], clsact[:, e, j, at:at + CLIPS],
                                  a2[:, c:c + D], j == 0, j == FJ - 1)
                last.then_inc(s_cy, 1)

        @block.scalar
        def _(act):
            act.wait_ge(s_const, 16)
            with act.Fori(0, GROUPS) as g:
                act.wait_ge(s_mel, g + 1)
                nc.scalar.activation(logmel, ps[0:MELS, 1, 0:GT], ACT.Ln,
                                     bias=const("tiny", MELS)).then_inc(s_log, 1)

            def evict(a, place, g, b, name):
                if a.owners[name] != "act":
                    return
                bank = fill(a, place, b, name)[1]
                filled(act, a, place, g, b, name)
                if name == "x":
                    nc.scalar.activation(xTa[:, 0:T], ps[0:DA, bank, 0:T], ACT.Identity,
                                         scale=column(LN_A), bias=column(LN_A + 1))
                    last = nc.scalar.activation(xTb[:, 0:T], ps[0:DB, bank, 128:128 + T], ACT.Identity,
                                                scale=column(LN_B, 1, DB), bias=column(LN_B + 1, 1, DB))
                elif name == "rb":
                    last = nc.scalar.activation(rTb, ps[0:DB, bank, 0:GT], ACT.Identity,
                                                scale=column(LN_B + 2, 1, DB), bias=column(LN_B + 3, 1, DB))
                elif name[0] in "qk":
                    dst = QT if name[0] == "q" else KT
                    tiles = tiles_of(a, name)
                    to = 0 if place == "start" else b + 1
                    if a.index:
                        t0, w = a.bank_tile(to, 0), a.tiles[0]
                        last = nc.scalar.copy(dst[0:w, t0:t0 + 3, :].rearrange("p m t -> p (m t)"),
                                              ps[0:w, bank, 0:3 * T])
                    else:
                        for j, tile in enumerate(tiles):
                            last = nc.scalar.activation(QT[:, tile, :], ps[:, bank, j * T:(j + 1) * T],
                                                        ACT.Identity, bias=column(BQ + tile))
                else:
                    src = ps[0:T, bank, 0:a.inner].rearrange("p (h x) -> p h x", h=a.heads)
                    last = nc.scalar.copy(vview(a, 0 if place == "start" else b + 1)[:, :, 0:a.hd], src)
                last.then_inc(s_xc, 1)

            def exp(a, g, s):
                act.wait_ge(s_sub, steps(a, g) + s + 1)
                nc.scalar.activation(probs(s), probs(s), ACT.Exp,
                                     scale=1.0 if a.index == 2 else float(a.hd) ** -0.5).then_inc(s_exp, 1)

            def clip_body(a, place, g, b, more):
                step = steps(a, g)
                clip = (a.index * GROUPS + g) * NB
                U = a.per_clip

                def evictions(at):
                    for name in fills_at(a, b, at) if more else []:
                        evict(a, place, g, b, name)

                def heads_copied(b):
                    act.wait_ge(s_ot, clip + b + 1)
                    wait(act, s_y, clip + b)
                    if a.index == 0:
                        o = OT[:, :, :].rearrange("p (k j) t -> p k (j t)", k=2)
                        last = nc.scalar.copy(o, ps[:, 4:6, 0:3 * T])
                    else:
                        for j, (_, w) in enumerate(out_runs(a)):
                            last = nc.scalar.copy(OT[0:w, j, :], heads_turned(a, j, w))
                    last.then_inc(s_otc, 1)

                for u in range(U):
                    s = b * U + u
                    act.wait_ge(s_pt, step + s + 1)
                    wait(act, s_o, step + s - 1)
                    nc.scalar.copy(probsT(s), ps[0:T, 4 + s % 2, 0:UNIT * T]).then_inc(s_ptc, 1)
                    evictions((u, 0))
                    if u == 0 and b and later(a, b - 1):
                        heads_copied(b - 1)
                    if u + 1 < U or U > 2 and more:
                        exp(a, g, s + 1)
                    if a.index == 1 and place != "first" and b == 1 and u == U - 1:
                        evict(a, place, g, b, "rb")
                    evictions((u, 1))
                if not later(a, b):
                    heads_copied(b)
                evictions("turned")
                if more and U == 2:
                    exp(a, g, s + 1)

            def gelu_tile(i, par):
                t = 2 * i + par
                act.wait_ge(s_m1p, t + 1)
                nc.scalar.activation(act1[:, par, :].rearrange("p (k x) -> p k x", k=2),
                                     ps[:, 1 + 2 * par:3 + 2 * par, 0:384], ACT.Gelu).then_inc(s_gel, 1)

            for a in LAYERS:
                if a.index == 0:
                    act.wait_ge(s_cols, 32)
                if a.index == 2:
                    act.wait_ge(s_tab, 1)
                    nc.scalar.activation(wgt[0:T, 1, :], gap[0:T, :], ACT.Exp).then_inc(s_gexp, 1)
                    with act.Fori(0, TILES // 2) as i:
                        gelu_tile(i, 0)
                        gelu_tile(i, 1)
                for b, name in a.order["start"]:
                    evict(a, "start", 0, b, name)
                exp(a, 0, 0)
                for b in range(NB):
                    clip_body(a, "first", 0, b, True)
                with act.Fori(1, GROUPS - 1) as g:
                    for b in range(NB):
                        clip_body(a, "mid", g, b, True)
                for b in range(NB):
                    clip_body(a, "last", GROUPS - 1, b, b < NB - 1)
                for b, name in a.order["tail"]:
                    evict(a, "tail", GROUPS - 1, b, name)

            act.wait_ge(s_f2, 48)
            with act.Fori(0, GROUPS) as g:
                for j in range(FJ):
                    act.wait_ge(s_fh, g * FJ + j + 1)
                    nc.scalar.activation(actF[:, j, :], ps[:, j % 2, 0:GT], ACT.Gelu,
                                         bias=b1c[:, j:j + 1]).then_inc(s_fg, 1)
            for e in range(NEXP):
                act.wait_ge(s_ch, e + 1)
                n = len(SERVES[e]) * CLIPS
                for j in range(FJ):
                    last = nc.scalar.activation(clsact[:, e, j, 0:n],
                                                ps[:, 2 * (e % 2) + j // 3, (j % 3) * 96:(j % 3) * 96 + n],
                                                ACT.Gelu, bias=a1bc[:, e * FJ + j:e * FJ + j + 1])
                last.then_inc(s_cg, 1)
            act.wait_ge(s_csub, 1)
            nc.scalar.activation(gate[:, 16:28], gate[:, 0:12], ACT.Exp).then_inc(s_cge, 1)

        @block.vector
        def _(dve):
            ch = Chain(dve, s_dve)
            V = nc.vector

            dve.wait_ge(s_cols, 32)
            dve.wait_ge(s_reat, 16)
            dve.wait_ge(s_anc, 16)
            for t in range(3):
                c = 384 + 13 * t
                prod = region1[0:64, 424 + 8 * t:430 + 8 * t]
                ch.after(V.tensor_tensor(prod, region1[0:64, c:c + 6], region1[0:64, c + 6:c + 12], ALU.mult))
                ch.after(V.tensor_reduce(mx[0:64, 0, t:t + 1], prod, AX.X, ALU.add))
                V.tensor_tensor(column(ANC + t, 1, 64), mx[0:64, 0, t:t + 1], region1[0:64, c + 12:c + 13], ALU.mult)
            V.tensor_reduce(column(HSC, 6), region1[:, 0:384].rearrange("p (j c) -> p j c", j=6),
                            AX.X, ALU.add).then_inc(s_set, 1)
            dve.wait_ge(s_comb, 1)
            V.tensor_copy(combined, ps[0:MELS, 7, 0:D]).then_inc(s_set, 1)
            dve.wait_ge(s_hsum, 1)
            ch.after(V.tensor_copy(rsum[:, 0, :], ps[:, 6, 0:6]))
            dve.wait_ge(s_w0, 48)
            V.tensor_tensor(wo0, wo0, rsum[:, 0, :].unsqueeze(2).to_broadcast([128, 6, D]),
                            ALU.mult).then_inc(s_set, 1)
            dve.wait_ge(s_const, 16)
            V.tensor_copy(run[:, :], const("region"))

            def squares(g):
                dve.wait_ge(s_dft, g + 1)
                ch.after(V.tensor_copy(spectrum, ps[0:2 * BINS, 0, 0:GT]))
                V.tensor_tensor(power, spectrum, spectrum, ALU.mult).then_inc(s_pow, 1)

            def token_rows(g):
                dve.wait_ge(s_tok, g + 1)
                for c in range(2):
                    last = V.tensor_tensor(hid[0:T, bass.ds(g * NB + 2 * c, 2), :],
                                           ps[0:T, 2 + c, 0:2 * D].rearrange("p (b d) -> p b d", b=2),
                                           rows[0:T, 0:D].unsqueeze(1).to_broadcast([T, 2, D]), ALU.add)
                last.then_inc(s_hid, 1)

            squares(0)
            with dve.Fori(0, GROUPS - 1) as g:
                ch.enter(g, 1)
                squares(g + 1)
                token_rows(g)
                ch.leave(GROUPS - 1)
            token_rows(GROUPS - 1)

            def measure(count, src, kind=2, free=1):
                mv = mv3[0:T, kind]
                wait(dve, s_var, count - 1)
                wait(dve, s_xn, count - free)
                settled(nc.vector)
                for b in range(NB):
                    last = V.bn_stats(stats[0:T, b, :], src(b))
                ch.after(last)
                settled(nc.vector)
                for b in range(NB):
                    last = V.bn_aggr(mv[:, b, :], stats[0:T, b, :])
                last.then_inc(s_var, 1)

            def apply(count, src, dst):
                dve.wait_ge(s_rstd, count)
                for b in range(NB):
                    last = V.tensor_scalar(dst(b), src(b), mv3[0:T, 2, b, 0:1], rstd3[0:T, 2, b:b + 1],
                                           ALU.subtract, ALU.mult)
                last.then_inc(s_xn, 1)

            def hid_of(g):
                return lambda b: hid[0:T, g * NB + b, :]

            def xres_of(g):
                return lambda b: xres[0:T, g * NB + b, :]

            def xn_of(b):
                return xn[0:T, b, :]

            def evict(a, place, g, b, name):
                if a.owners[name] != "dve":
                    return
                bank = fill(a, place, b, name)[1]
                filled(dve, a, place, g, b, name)
                if name == "x":
                    sa, sb_ = ps[0:DA, bank, 0:T], ps[0:DB, bank, 128:128 + T]
                    V.tensor_copy(xTa[:, 0:T], sa)
                    last = V.tensor_copy(xTb[:, 0:T], sb_)
                elif name == "ra":
                    last = V.tensor_scalar(rTa, ps[0:DA, bank, 0:GT], column(LN_A + 2), column(LN_A + 3),
                                           ALU.mult, ALU.add)
                elif name == "lg":
                    last = V.tensor_copy(table(1), ps[0:T, bank, 0:NB * E])
                elif name == "ct":
                    V.tensor_copy(table(5)[:, 0:E], run[0:T, :])
                    last = V.tensor_copy(route[0:T, 9 * NB * E:11 * NB * E], ps[0:T, bank, 0:2 * NB * E])
                elif name[0] == "k":
                    tiles = tiles_of(a, name)
                    if a.index == 0:
                        n, t0 = len(tiles), tiles[0]
                        last = V.tensor_tensor(KT[:, t0:t0 + n, :],
                                               ps[:, bank, 0:n * T].rearrange("p (m t) -> p m t", m=n),
                                               column(BK + t0, n).unsqueeze(2).to_broadcast([128, n, T]), ALU.add)
                    else:
                        for j, tile in enumerate(tiles):
                            w = a.tiles[tile]
                            to = a.bank_tile(0 if place == "start" else b + 1, tile)
                            last = V.tensor_scalar(KT[0:w, to, :], ps[0:w, bank, j * T:(j + 1) * T],
                                                   float(a.hd) ** -0.5, column(ANC + tile, 1, w),
                                                   ALU.mult, ALU.add)
                else:
                    n = a.heads // a.halves
                    half, w = int(name[1]), n * a.hd
                    src = ps[0:T, bank, 0:w].rearrange("p (h x) -> p h x", h=n)
                    dst = vview(a, 0)[:, half * n:(half + 1) * n, 0:a.hd]
                    c = 2 * D + half * w
                    last = V.tensor_tensor(dst, src, rows[0:T, c:c + w].rearrange("p (h x) -> p h x", h=n),
                                           ALU.add)
                last.then_inc(s_xd, 1)

            def less_max(a, g, s):
                step = steps(a, g)
                dve.wait_ge(s_s, step + s + 1)
                m = mx[0:T, s % 2, 0:UNIT]
                wait(dve, s_sub, step + s - 1)
                ch.after(V.tensor_reduce(m, scores_view(s), AX.X, ALU.max))
                wait(dve, s_pt, step + s - 1)
                V.tensor_tensor(three(probs(s)), scores_view(s),
                                m.unsqueeze(2).to_broadcast([T, UNIT, T]), ALU.subtract).then_inc(s_sub, 1)

            def clip_body(a, place, g, b, more):
                step = steps(a, g)
                clip = (a.index * GROUPS + g) * NB
                U = a.per_clip
                ahead = place != "last"
                routing = a.index == 1 and place != "first"
                routed = routed_group(place, g)
                one = LAYERS[1]

                def evictions(at):
                    for name in fills_at(a, b, at) if more else []:
                        evict(a, place, g, b, name)

                def heads_normalized(s):
                    dve.wait_ge(s_o, step + s + 1)
                    o = heads_out(a)
                    r = rsum[0:T, s % 2, 0:UNIT]
                    wait(dve, s_on, step + s - 1)
                    ch.after(V.reciprocal(r, o[:, :, a.hd]))
                    wait(dve, s_ot, clip + b)
                    c = unit_heads(a, s)[0] * a.hd
                    V.tensor_tensor(three(osb[0:T, c:c + UNIT * a.hd]), o[:, :, 0:a.hd],
                                    r.unsqueeze(2).to_broadcast([T, UNIT, a.hd]), ALU.mult).then_inc(s_on, 1)

                def early_work():
                    if a.index == 0 and not ahead and b == 2:
                        dve.wait_ge(s_xn, norm(one, "start", 0, "own"))
                        measure(norm(one, "start", 0, "next"), xres_of(0))
                    if a.index == 2 and ahead and b == 0:
                        gather_rows(g + 1)
                    if a.index == 1 and ahead and b == 1:
                        measure(norm(a, place, g, "own"), hid_of(g + 1), 0, 2)
                    if routing and b == 0:
                        dve.wait_ge(s_hup, (GROUPS + routed + 1) * NB)
                        measure(norm(a, place, g, "route"), xres_of(routed), 1, 2)
                    if a.index == 1 and ahead and b == 2:
                        dve.wait_ge(s_xn, norm(a, place, g, "own"))
                        measure(norm(a, place, g, "next"), xres_of(g + 1), 2, 2)
                    if routing and b == 2:
                        evict(a, place, g, 2, "lg")
                        took(dve, a, place, g, 2, "lg")
                        first_choice()
                    if routing and b == 3:
                        second_choice(routed)

                def middle_work():
                    if a.index == 0 and ahead and b == 1:
                        measure(norm(a, place, g, "next"), hid_of(g + 1))
                    if a.index == 0 and not ahead and b == 0:
                        dve.wait_ge(s_hup, NB)
                        measure(norm(one, "start", 0, "own"), hid_of(0), 0)
                    if a.index == 2 and not ahead and b == 2:
                        apply(NORMS[3] + 1, hid_of(0), xn_of)

                def late_work():
                    if routing and b == 3:
                        evict(a, place, g, 3, "ct")
                        took(dve, a, place, g, 3, "ct")
                        rows_before()
                        rows_found(routed)
                    if a.index == 2 and ahead and b == 1:
                        mix(g + 1)
                        measure(norm(a, place, g, "next"), hid_of(g + 1))
                    if a.index == 2 and not ahead and b == 1:
                        dve.wait_ge(s_hup, 2 * CLIPS + NB)
                        measure(NORMS[3] + 1, hid_of(0))

                def add_heads(b):
                    dve.wait_ge(s_y, clip + b + 1)
                    if a.index == 0:
                        dve.wait_ge(s_res, g + 1)
                    dst = xres[0:T, g * NB + b, :] if a.index == 1 else hid[0:T, g * NB + b, :]
                    V.tensor_tensor(dst, ps[0:T, 7, 0:D], dst, ALU.add).then_inc(s_hup, 1)

                for u in range(U):
                    s = b * U + u
                    evictions((u, 0))
                    if u < U - 1:
                        if u + 2 < U or more and U > 2:
                            less_max(a, g, s + 2)
                        heads_normalized(s)
                    else:
                        heads_normalized(s)
                        if more:
                            less_max(a, g, s + (2 if U > 2 else 1))
                    if routing and b == 1 and u == U - 1:
                        evict(a, place, g, b, "ra")
                    if u == 0 and b and later(a, b - 1):
                        add_heads(b - 1)
                    evictions((u, 1))
                    if u == 0:
                        early_work()
                    if u == U // 2 - 1:
                        middle_work()
                if more and U == 2:
                    less_max(a, g, s + 2)
                evictions("turned")
                if not later(a, b):
                    add_heads(b)
                late_work()

            def table(k, n=NB * E):
                return route[0:T, k * NB * E:k * NB * E + n]

            def per_expert(x):
                return x.rearrange("p (b e) -> p b e", b=NB)

            first, other = table(7), table(8)
            number = rstd2[0:T, 0:NB]

            best = kept[0:T, 0:NB]
            second = kept[0:T, NB:2 * NB]

            def one_hot(values, top, dst):
                rev = const("rev", T)
                ch.after(V.tensor_reduce(top, per_expert(values), AX.X, ALU.max))
                ch.after(V.tensor_tensor(per_expert(table(2)), per_expert(values),
                                         top.unsqueeze(2).to_broadcast([T, NB, E]), ALU.is_equal))
                ch.after(V.tensor_tensor(table(2), table(2), rev, ALU.mult))
                ch.after(V.tensor_reduce(number, per_expert(table(2)), AX.X, ALU.max))
                ch.after(V.tensor_tensor(per_expert(dst), per_expert(rev),
                                         number.unsqueeze(2).to_broadcast([T, NB, E]), ALU.is_equal))

            def first_choice():
                one_hot(table(1), best, first)

            def second_choice(g):
                ch.after(V.scalar_tensor_tensor(table(3), first, -3.0e38, table(1), ALU.mult, ALU.add))
                one_hot(table(3), second, other)
                V.tensor_copy(hot[0:T, 0, bass.ds(g * NB, NB), :], per_expert(first))
                V.tensor_copy(hot[0:T, 1, bass.ds(g * NB, NB), :], per_expert(other))
                V.tensor_tensor(gap[0:T, bass.ds(g * NB, NB)], second, best, ALU.subtract)
                V.tensor_tensor(table(0), first, other, ALU.add).then_inc(s_hot, 1)

            def rows_before():
                before, totals, base = table(9), per_expert(table(10)), per_expert(table(5))
                for b in range(1, NB):
                    ch.after(V.tensor_tensor(base[:, b, :], base[:, b - 1, :], totals[:, b - 1, :], ALU.add))
                ch.after(V.tensor_tensor(run[0:T, :], base[:, NB - 1, :], totals[:, NB - 1, :], ALU.add))
                ch.after(V.tensor_tensor(table(6), table(5), before, ALU.add))

            def rows_found(g):
                for k, h in ((0, first), (1, other)):
                    ch.after(V.tensor_tensor(table(2), table(6), h, ALU.mult))
                    ch.after(V.tensor_reduce(number, per_expert(table(2)), AX.X, ALU.add))
                    V.tensor_copy(pos[0:T, k, bass.ds(g * NB, NB)], number)
                    last = V.tensor_copy(idx[0:T, k, :], number)
                    if k == 0:
                        ch.after(last)
                last.then_inc(s_idx, 1)

            def tables():
                P = slice(0, T)
                count, tiles, end, adjust = (tl[P, k, :] for k in range(4))
                ch.after(V.tensor_tensor(count, run[P, :], const("region", T), ALU.subtract))
                sp8 = spread[P, :].rearrange("p (e k) -> p e k", e=E)
                ch.after(V.tensor_tensor(sp8, count.unsqueeze(2).to_broadcast([T, E, 32]),
                                         const("bounds", T).rearrange("p (e k) -> p e k", e=E), ALU.is_gt))
                ch.after(V.tensor_reduce(tiles, sp8, AX.X, ALU.add))
                ch.after(V.tensor_copy(end, tiles))
                for e in range(1, E):
                    ch.after(V.tensor_tensor(end[:, e:e + 1], end[:, e:e + 1], end[:, e - 1:e], ALU.add))
                ch.after(V.tensor_tensor(adjust, end, tiles, ALU.subtract))
                start = tiles
                ch.after(V.tensor_copy(start, adjust))
                ch.after(V.scalar_tensor_tensor(adjust, adjust, 128.0, const("region", T), ALU.mult, ALU.subtract))
                n = TILES + LOADED
                shape = [1, n, E]

                def grid(x):
                    return x.rearrange("p (t e) -> p t e", t=n)

                t_ = grid(const("tile", 1))
                mine, work, work2 = (grid(tabf[0:1, k, :]) for k in range(3))
                ch.after(V.tensor_tensor(work, t_, start[0:1, :].unsqueeze(1).to_broadcast(shape), ALU.is_ge))
                ch.after(V.tensor_tensor(work2, t_, end[0:1, :].unsqueeze(1).to_broadcast(shape), ALU.is_lt))
                ch.after(V.tensor_tensor(mine, work, work2, ALU.mult))
                ch.after(V.scalar_tensor_tensor(work, t_, 128.0, adjust[0:1, :].unsqueeze(1).to_broadcast(shape),
                                                ALU.mult, ALU.subtract))
                ch.after(V.tensor_tensor(work, work, mine, ALU.mult))
                ch.after(V.tensor_reduce(work2[:, :, 0], work, AX.X, ALU.add))
                ch.after(V.tensor_copy(tab[0:1, 0, :], work2[:, :, 0]))
                ch.after(V.tensor_tensor(work, grid(const("tile_e", 1)), mine, ALU.mult))
                ch.after(V.tensor_reduce(work2[:, :, 0], work, AX.X, ALU.add))
                V.tensor_copy(tab[0:1, 1, :], work2[:, :, 0]).then_inc(s_tab, 1)

            def places():
                P = slice(0, T)
                adjust = tl[P, 3, :]
                for k in range(2):
                    big = spread[P, :].rearrange("p (b e) -> p b e", b=CLIPS)
                    ch.after(V.tensor_tensor(big, hot[P, k, :, :],
                                             adjust.unsqueeze(1).to_broadcast([T, CLIPS, E]), ALU.mult))
                    ch.after(V.tensor_reduce(shift[P, :], big, AX.X, ALU.add))
                    ch.after(V.tensor_tensor(pos[P, k, :], pos[P, k, :], shift[P, :], ALU.add))
                dve.wait_ge(s_gexp, 1)
                ch.after(V.tensor_scalar(wgt[P, 0, :], wgt[P, 1, :], 1.0, None, ALU.add))
                ch.after(V.reciprocal(wgt[P, 0, :], wgt[P, 0, :]))
                ch.after(V.tensor_tensor(wgt[P, 1, :], wgt[P, 1, :], wgt[P, 0, :], ALU.mult))

            def mixture():
                def turned(t, par):
                    dve.wait_ge(s_mt, t + 1)
                    V.tensor_scalar(xsT[:, par, 0:128], ps[:, 0, 0:128], column(LN_A + 2), column(LN_A + 3),
                                    ALU.mult, ALU.add)
                    V.tensor_scalar(xsT[0:DB, par, 128:256], ps[0:DB, 0, 128:256], column(LN_B + 2, 1, DB),
                                    column(LN_B + 3, 1, DB), ALU.mult, ALU.add).then_inc(s_mtc, 1)

                def tile(i, par):
                    t = 2 * i + par
                    turned(t + AHEAD, par)
                    dve.wait_ge(s_gt, t + 1)
                    V.tensor_copy(act1T[:, par, :].rearrange("p (k x) -> p k x", k=2),
                                  ps[:, 5:7, 0:384]).then_inc(s_gtc, 1)
                    dve.wait_ge(s_m2p, t + 1)
                    wait(dve, s_st[par], 16 * i)
                    V.tensor_copy(ys[:, par, :], ps[:, 7, 0:D]).then_inc(s_ys, 1)

                turned(0, 0)
                turned(1, 1)
                places()
                tile(0, 0)
                tile(0, 1)
                with dve.Fori(1, TILES // 2) as i:
                    tile(i, 0)
                    tile(i, 1)

            def gather_rows(g):
                V.tensor_copy(idy[0:T, :, :], pos[0:T, :, bass.ds(g * NB, NB)]).then_inc(s_idy, 1)

            def mix(g):
                for k in range(2):
                    for b in range(NB):
                        dve.wait_ge(s_got[k * NB + b], 16 * (g + 1))
                        h = hid[0:T, g * NB + b, :]
                        last = V.scalar_tensor_tensor(h, got[0:T, k, b, :], wgt[0:T, k, bass.ds(g * NB + b, 1)],
                                                      h, ALU.mult, ALU.add)
                    if k == 0:
                        ch.after(last)
                ch.after(last)

            for a in LAYERS:
                if a.index == 2:
                    tables()
                    mixture()
                    dve.wait_ge(s_m2p, TILES)
                    dve.wait_ge(s_res, 2 * GROUPS)
                dve.wait_ge(s_hid, GROUPS)
                if a.index:
                    dve.wait_ge(s_hup, a.index * CLIPS)
                for b in range(2 if a.index else 1):
                    V.memset(vview(a, b)[:, :, a.hd:a.hd + 1], 1.0)
                n = norm(a, "start", 0, "next")
                if a.index != 1:
                    if a.index == 2:
                        gather_rows(0)
                        mix(0)
                    measure(n, hid_of(0))
                for b, name in a.order["start"]:
                    evict(a, "start", 0, b, name)
                less_max(a, 0, 0)
                less_max(a, 0, 1)
                for b in range(NB):
                    clip_body(a, "first", 0, b, True)
                with dve.Fori(1, GROUPS - 1) as g:
                    ch.enter(g, CHAIN[a.index], 1)
                    for b in range(NB):
                        clip_body(a, "mid", g, b, True)
                    ch.leave(GROUPS - 2)
                for b in range(NB):
                    clip_body(a, "last", GROUPS - 1, b, b < NB - 1)
                if a.index == 1:
                    g = GROUPS - 1
                    dve.wait_ge(s_hup, (GROUPS + g + 1) * NB)
                    measure(norm(a, "tail", g, "route"), xres_of(g), 1)
                    evict(a, "tail", g, 1, "ra")
                    evict(a, "tail", g, 2, "lg")
                    took(dve, a, "tail", g, 2, "lg")
                    first_choice()
                    second_choice(g)
                    evict(a, "tail", g, 3, "ct")
                    took(dve, a, "tail", g, 3, "ct")
                    rows_before()
                    rows_found(g)
                    V.tensor_copy(padrow[0:1, :], run[0:1, :]).then_inc(s_padrow, 1)

            dve.wait_ge(s_hup, 3 * CLIPS)
            dve.wait_ge(s_f2, 48)

            def rows_turned(g):
                dve.wait_ge(s_lx, g + 1)
                V.tensor_copy(xTa[:, :], ps[:, 4, 0:GT])
                ch.after(V.tensor_copy(xTb[:, :], ps[0:DB, 5, 0:GT]))
                V.tensor_copy(clsa[:, :, bass.ds(g * NB, NB)],
                              xTa[:, :].rearrange("p (b t) -> p t b", t=T)[:, 0:NCLS, :]).then_inc(s_lxd, 1)
                V.tensor_copy(clsb[:, :, bass.ds(g * NB, NB)],
                              xTb[:, :].rearrange("p (b t) -> p t b", t=T)[:, 0:NCLS, :]).then_inc(s_cls, 1)

            def last_group(g, more):
                if more:
                    n = NORMS[3] + g + 2
                    measure(n, hid_of(g + 1))
                    dve.wait_ge(s_lx, g + 1)
                    apply(n, hid_of(g + 1), xn_of)
                    rows_turned(g + 1)
                dve.wait_ge(s_res, 2 * GROUPS + g + 1)
                for b in range(NB):
                    dve.wait_ge(s_fy, g * NB + b + 1)
                    V.tensor_tensor(fin[0:T, b, :], ps[0:T, 6 + b % 2, 0:D],
                                    fin[0:T, b, :], ALU.add).then_inc(s_ft, 1)

            rows_turned(0)
            last_group(0, True)
            with dve.Fori(1, GROUPS - 1) as g:
                ch.enter(g, CHAIN[3], 1)
                last_group(g, True)
                ch.leave(GROUPS - 2)
            last_group(GROUPS - 1, False)

            def pairs(c):
                return gate[:, c:c + 12].rearrange("p (i s) -> p i s", s=2)

            def wide(x):
                return x.unsqueeze(2).to_broadcast([CLIPS, NCLS, 2])

            dve.wait_ge(s_cgate, 1)
            logits = ps[0:CLIPS, 4, 0:12].rearrange("p (i s) -> p i s", s=2)
            top, total, least = gate[:, 32:38], gate[:, 40:46], gate[:, 48:54]
            ch.after(V.tensor_reduce(top, logits, AX.X, ALU.max))
            V.tensor_tensor(pairs(0), logits, wide(top), ALU.subtract).then_inc(s_csub, 1)
            dve.wait_ge(s_cge, 1)
            ch.after(V.tensor_reduce(total, pairs(16), AX.X, ALU.add))
            ch.after(V.reciprocal(total, total))
            ch.after(V.tensor_tensor(pairs(16), pairs(16), wide(total), ALU.mult))
            ch.after(V.tensor_reduce(least, pairs(16), AX.X, ALU.min))
            ch.after(V.tensor_tensor(pairs(56), pairs(16), wide(least), ALU.is_gt))
            ch.after(V.tensor_tensor(pairs(16), pairs(16), pairs(56), ALU.mult))
            ch.after(V.tensor_reduce(total, pairs(16), AX.X, ALU.add))
            ch.after(V.tensor_scalar(total, total, 1e-6, None, ALU.max))
            ch.after(V.reciprocal(total, total))
            ch.after(V.tensor_tensor(pairs(16), pairs(16), wide(total), ALU.mult))
            dve.wait_ge(s_clsh, 16 * NCLS)
            for i in range(NCLS):
                dve.wait_ge(s_cy, i + 1)
                for s in range(2):
                    c = (1 + PAIR[i][1 - s]) * D
                    last = V.tensor_tensor(clso[:, i, s, :], ps[0:CLIPS, 6 + i % 2, s * D:(s + 1) * D],
                                           rows2[0:CLIPS, c:c + D], ALU.add)
                last.then_inc(s_ct, 1)
                dve.wait_ge(s_ct, i + 1)
                for s in range(2):
                    last = V.scalar_tensor_tensor(clsh[:, i, :], clso[:, i, s, :],
                                                  gate[:, 16 + 2 * i + s:17 + 2 * i + s],
                                                  clsh[:, i, :], ALU.mult, ALU.add)
                    if s == 0:
                        ch.after(last)
                last.then_inc(s_cfin, 1)

        @block.gpsimd
        def _(pool):
            ch = Chain(pool, s_poolc)
            G = nc.gpsimd
            G.memset(zeros[:, :], 0.0).then_inc(s_setp, 1)
            pool.wait_ge(s_const, 16)
            pool.wait_ge(s_cols, 32)
            pool.wait_ge(s_hid, GROUPS)

            def deviations(count, kind=2):
                r = rstd3[0:T, kind]
                pool.wait_ge(s_var, count)
                ch.after(G.tensor_tensor(r, mv3[0:T, kind, :, 1], const("eps", T), ALU.add))
                G.tensor_tensor(r, r, const("half", T), ALU.pow).then_inc(s_rstd, 1)

            def wide(x):
                return x.unsqueeze(2).to_broadcast([T, NB, D])

            def hid4(g):
                return hid[0:T, bass.ds(g * NB, NB), :]

            def xres4(g):
                return xres[0:T, bass.ds(g * NB, NB), :]

            def normalized(count, kind, src, dst, place):
                pool.wait_ge(s_rstd, count)
                settled(nc.gpsimd, place)
                ch.after(G.tensor_tensor(dst, src, wide(mv3[0:T, kind, :, 0]), ALU.subtract))
                settled(nc.gpsimd, place)
                G.tensor_tensor(dst, dst, wide(rstd3[0:T, kind]), ALU.mult).then_inc(s_xn, 1)

            def norm_next(a, place, g):
                count = norm(a, place, g, "next")
                deviations(count)
                filled(pool, a, place, g, 2, "x")
                normalized(count, 2, xres4(g + 1) if a.index == 1 else hid4(g + 1), xn[0:T, :, :], 4)

            def norm_route(a, place, g):
                h = routed_group(place, g)
                count = norm(a, place, g, "route")
                deviations(count, 1)
                normalized(count, 1, xres4(h), xrow[0:T, :, :], 5)

            def gather(g):
                pool.wait_ge(s_idy, g + 1)
                settled(nc.gpsimd, 0)
                for k in range(2):
                    for b in range(NB):
                        G.indirect_dma_start(
                            out=got[0:T, k, b, :], out_offset=None, in_=expert_out,
                            in_offset=bass.IndirectOffsetOnAxis(ap=idy[0:T, k, b:b + 1], axis=0),
                        ).then_inc(s_got[k * NB + b], 16)

            def add_rows(g, x):
                four = hid[0:T, bass.ds(g * NB, NB), :]
                G.tensor_tensor(four, four, x, ALU.add).then_inc(s_res, 1)

            def with_bias(g, count):
                pool.wait_ge(s_xn, count)
                settled(nc.gpsimd, 1)
                add_rows(g, rows[0:T, D:2 * D].unsqueeze(1).to_broadcast([T, NB, D]))

            def scatter(g):
                pool.wait_ge(s_idx, g + 1)
                settled(nc.gpsimd, 2)
                for k in range(2):
                    for b in range(NB):
                        G.indirect_dma_start(
                            out=routed, in_=xrow[0:T, b, :], in_offset=None,
                            out_offset=bass.IndirectOffsetOnAxis(ap=idx[0:T, k, b:b + 1], axis=0),
                        ).then_inc(s_scat[k * NB + b], 16)
                for k in range(2 * NB):
                    pool.wait_ge(s_scat[k], 16 * (g + 1))

            def group_body(a, place, g):
                if a.index == 0:
                    if place != "last":
                        norm_next(a, place, g)
                        with_bias(g + 1, norm(a, place, g, "next"))
                    else:
                        one = LAYERS[1]
                        own, count = norm(one, "start", 0, "own"), norm(one, "start", 0, "next")
                        deviations(own, 0)
                        normalized(own, 0, hid4(0), xres4(0), 4)
                        deviations(count)
                        filled(pool, a, place, g, 2, "x")
                        normalized(count, 2, xres4(0), xn[0:T, :, :], 4)
                elif a.index == 1:
                    if place != "first":
                        norm_route(a, place, g)
                    if place in ("first", "mid"):
                        own = norm(a, place, g, "own")
                        deviations(own, 0)
                        normalized(own, 0, hid4(g + 1), xres4(g + 1), 4)
                        norm_next(a, place, g)
                    if place != "first":
                        h = routed_group(place, g)
                        add_rows(h, xres4(h))
                        scatter(h)
                elif place != "last":
                    gather(g + 1)
                    norm_next(a, place, g)
                else:
                    deviations(NORMS[3] + 1)

            for a in LAYERS:
                if a.index == 2:
                    for k in range(2):
                        pool.wait_ge(s_st[k], 16 * (TILES // 2))
                    gather(0)
                count = norm(a, "start", 0, "next")
                if a.index != 1:
                    deviations(count)
                    normalized(count, 2, hid4(0), xn[0:T, :, :], 4)
                if a.index == 0:
                    with_bias(0, count)
                group_body(a, "first", 0)
                with pool.Fori(1, GROUPS - 1) as g:
                    ch.enter(g, CHAIN_POOL[a.index], 1)
                    group_body(a, "mid", g)
                    ch.leave(GROUPS - 2)
                group_body(a, "last", GROUPS - 1)
                if a.index == 1:
                    group_body(a, "tail", GROUPS - 1)
            pool.wait_ge(s_f2, 48)

            def last_rows(g):
                wait(pool, s_out, 16 * g)
                settled(nc.gpsimd, 3)
                G.tensor_tensor(fin[0:T, :, :], hid[0:T, bass.ds(g * NB, NB), :],
                                rows2[0:T, 0:D].unsqueeze(1).to_broadcast([T, NB, D]), ALU.add).then_inc(s_res, 1)

            last_rows(0)
            with pool.Fori(1, GROUPS) as g:
                ch.enter(g, CHAIN_POOL[3], 1)
                deviations(NORMS[3] + g + 1)
                last_rows(g)
                ch.leave(GROUPS - 1)

    return nc


def fold(w):
    n = w.shape[1]
    out = np.zeros((128, 2 * n), np.float32)
    out[:, :n] = w[:DA]
    out[:DB, n:] = w[DA:]
    return out


def placed(w, a):
    out = np.zeros((w.shape[0], len(a.tiles), a.tiles[0]), np.float32)
    for h in range(a.heads):
        tile, p = a.head_at(h)
        out[:, tile, p:p + a.hd] = w[:, h * a.hd:(h + 1) * a.hd]
    return out.reshape(w.shape[0], a.qk)


def lay_out(x):
    f = {k: np.asarray(v) for k, v in x.items()}
    c = constants()
    d = {"consts": np.concatenate(list(c.values()), 1)}
    clips = f["x"][:, :STEP * T].reshape(CLIPS, T, STEP)[:, :, :FRAME]
    d["frames"] = clips.transpose(2, 0, 1).reshape(FRAME, TOKENS)
    j = np.arange(FRAME)
    window = 0.54 - 0.46 * np.cos(2 * np.pi * j / (FRAME - 1))
    angle = 2 * np.pi * (np.outer(j, np.arange(BINS)) % FRAME) / FRAME
    d["dft"] = (window[:, None] * np.concatenate([np.cos(angle), -np.sin(angle)], 1)).astype(np.float32)
    mel = f["L0_tok_mel_filters"].T
    d["melw"] = np.concatenate([mel, mel], 0)
    d["dct"], d["wproj"] = f["L0_tok_dct"], f["L0_tok_w_proj"]
    bqkv = f["L0_attn_b_qkv"]
    d["rows"] = np.concatenate([f["L0_tok_b_proj"], f["L0_attn_b_out"], bqkv[1536:]])[None]
    cols = np.zeros((128, 42), np.float32)
    for k in range(2):
        cols[:, 6 * k:6 * k + 6] = placed(bqkv[None, 768 * k:768 * (k + 1)], LAYERS[0]).reshape(6, 128).T
    ln = np.stack([f["L0_ffn_" + k] for k in ("ln1_g", "ln1_b", "ln2_g", "ln2_b")], 1)
    cols[:, 12:16], cols[:DB, 16:20] = ln[:DA], ln[DA:]
    cols[:, 26:34], cols[:DB, 34:42] = f["L0_ffn_Wrouter"][:DA], f["L0_ffn_Wrouter"][DA:]
    d["cols"] = cols
    d["reat"] = f["L0_attn_reattn_weights"].reshape(6, 128, 64).transpose(1, 0, 2).reshape(128, 384)
    anchor = np.concatenate([f["L1_attn_anchor_w"].reshape(D, 6), np.repeat(f["L1_attn_anchors"], 32, 0),
                             np.repeat(f["L1_attn_lam"], 32)[:, None]], 1)
    d["anchor"] = placed(anchor.T, LAYERS[2]).reshape(13, 3, 64).transpose(2, 1, 0).reshape(64, 39)
    w = f["L0_attn_w_qkv"]
    w = np.concatenate([placed(w[:, :768], LAYERS[0]), placed(w[:, 768:1536], LAYERS[0]), w[:, 1536:]], 1)
    d["w0a"], d["w0b"] = w[:DA], w[DA:]
    d["wo0"] = f["L0_attn_w_out"].reshape(6, 128, D).transpose(1, 0, 2).reshape(128, 6 * D)
    w = f["L0_ffn_Wqkv"]
    w = np.concatenate([placed(w[:, :D], LAYERS[1]), placed(w[:, D:2 * D], LAYERS[1]), w[:, 2 * D:]], 1)
    d["w1"] = np.concatenate([fold(w), fold(f["L0_ffn_Wproj"])], 1)
    w = np.concatenate([placed(f["L1_attn_Wq"].T, LAYERS[2]), placed(f["L1_attn_Wk"].T, LAYERS[2]),
                        f["L1_attn_Wv"].T], 1)
    d["w2"] = np.concatenate([fold(w), fold(f["L1_attn_Wo"].T)], 1)
    w = f["L0_ffn_W1"].transpose(1, 0, 2).reshape(D, E * FF)
    d["m1a"], d["m1b"] = w[:DA], w[DA:]
    d["m2"] = f["L0_ffn_W2"].reshape(E, FJ, 128, D).transpose(2, 0, 1, 3).reshape(128, E * FJ * D)
    w = f["L1_ffn_A1_W"].transpose(1, 0, 2).reshape(D, NEXP * FF)
    d["a1"] = fold(w)
    d["f"] = np.concatenate([fold(f["L1_ffn_moe0_W1"]),
                             f["L1_ffn_moe0_W2"].reshape(FJ, 128, D).transpose(1, 0, 2).reshape(128, FJ * D)], 1)
    d["a2"] = f["L1_ffn_A2_W"].reshape(NEXP, FJ, 128, D).transpose(2, 0, 1, 3).reshape(128, NEXP * FJ * D)
    d["rows2"] = np.concatenate([f["L1_ffn_moe0_b2"], f["L1_ffn_A2_b"].reshape(-1)])[None]
    last = np.zeros((128, 80), np.float32)
    last[:, 0:6] = f["L1_ffn_moe0_b1"].reshape(6, 128).T
    last[:, 6:36] = f["L1_ffn_A1_b"].reshape(30, 128).T
    g = f["L1_ffn_G_W"].transpose(1, 0, 2).reshape(D, 2 * NCLS)
    last[:, 40:52], last[:DB, 60:72] = g[:DA], g[DA:]
    d["lastcols"] = last
    return {k: np.ascontiguousarray(v) for k, v in d.items()}


def kernel(**inputs):
    import concourse.bacc as bacc
    from concourse.bass_utils import run_bass_kernel_spmd

    nc = bacc.Bacc("TRN2", target_bir_lowering=False, num_devices=1)
    arrays, aps = {}, {}
    for name, a in lay_out(inputs).items():
        arrays[f"in_{name}"] = a
        aps[name] = nc.dram_tensor(f"in_{name}", a.shape, mybir.dt.from_np(a.dtype), kind="ExternalInput").ap()
    out = nc.dram_tensor("out", (CLIPS, T, D), F32, kind="ExternalOutput").ap()
    build(nc, aps, out)
    r = run_bass_kernel_spmd(nc, [arrays], core_ids=[0])
    return r.results[0]["out"]
```
